# Optimizing a Trainium2 kernel written in Bass

```python
import numpy as np
import jax
import jax.numpy as jnp

def _softmax(x, axis=-1):
    return jax.nn.softmax(x, axis=axis)

def _gelu(x):
    return jax.nn.gelu(x, approximate=True)

def _silu(x):
    return jax.nn.silu(x)

def _sigmoid(x):
    return jax.nn.sigmoid(x)

def _layernorm(x, axis=-1, eps=1e-05):
    m = jnp.mean(x, axis=axis, keepdims=True)
    v = jnp.var(x, axis=axis, keepdims=True)
    return (x - m) / jnp.sqrt(v + eps)

def _scatter_add(tgt, idx, src, axis=0):
    return tgt.at[idx].add(src)

def _segment_sum(src, seg, n):
    return jax.ops.segment_sum(src, seg, n)
kernel_name = 'mk_sandwich_d1_jaxref_r4_909d2b'

def setup_inputs(seed: int=0):
    np.random.seed(seed)
    _w = jnp.asarray

    def _L0_attn_setup():
        import math
        import jax, jax.numpy as jnp
        import numpy as np

        def _expmap0(u):
            u0 = u[..., :1]
            us = u[..., 1:]
            mink = -u0 * u0 + jnp.sum(us * us, axis=-1, keepdims=True)
            nomin = jnp.sqrt(jnp.maximum(mink, 1e-08))
            r = jnp.sinh(nomin) * u / nomin
            space = r[..., 1:]
            time = jnp.sqrt(1.0 + jnp.sum(space * space, axis=-1, keepdims=True))
            return jnp.concatenate([time, space], axis=-1)
        key = jax.random.key(seed)
        B, T, E, H = (2, 256, 256, 16)
        ks = jax.random.split(key, 8)
        s = 0.02
        return {'x': jax.random.normal(ks[0], (B, T, E), jnp.float32), 'Wqkv': jax.random.normal(ks[1], (3 * E, E), jnp.float32) * s, 'bqkv': jnp.zeros((3 * E,), jnp.float32), 'Wout': jax.random.normal(ks[2], (E, E), jnp.float32) * s, 'bout': jnp.zeros((E,), jnp.float32), 'Wimp': jax.random.normal(ks[3], (1, E), jnp.float32) * s, 'bimp': jnp.zeros((1,), jnp.float32), 'Walpha': jax.random.normal(ks[4], (H, E), jnp.float32) * s, 'balpha': jnp.zeros((H,), jnp.float32), 'spike_threshold': jnp.asarray(0.5, jnp.float32), 'log_k': jnp.full((H,), 0.54, jnp.float32), 'qk_scale': jnp.asarray(0.1, jnp.float32)}
    _L0_attn_in = _L0_attn_setup()

    def _L0_ffn_setup():
        import jax, jax.numpy as jnp
        import numpy as np
        LN_EPS = 1e-12
        key = jax.random.key(seed)
        ks = jax.random.split(key, 8)
        B, S, H, I, E = (4, 512, 256, 1024, 8)
        sH = 1.0 / np.sqrt(H)
        sI = 1.0 / np.sqrt(I)
        return {'hidden_states': jax.random.normal(ks[0], (B, S, H), dtype=jnp.float32), 'Wr': jax.random.uniform(ks[1], (E, H), jnp.float32, -sH, sH), 'W1': jax.random.uniform(ks[2], (E, H, I), jnp.float32, -sH, sH), 'b1': jax.random.uniform(ks[3], (E, I), jnp.float32, -sH, sH), 'Wo': jax.random.uniform(ks[4], (I, H), jnp.float32, -sI, sI), 'bo': jax.random.uniform(ks[5], (H,), jnp.float32, -sI, sI), 'gamma': jnp.ones((H,), jnp.float32), 'beta': jnp.zeros((H,), jnp.float32)}
    _L0_ffn_in = _L0_ffn_setup()
    _d = {'L0_attn_x': _L0_attn_in['x'], 'L0_attn_Wqkv': _L0_attn_in['Wqkv'], 'L0_attn_bqkv': _L0_attn_in['bqkv'], 'L0_attn_Wout': _L0_attn_in['Wout'], 'L0_attn_bout': _L0_attn_in['bout'], 'L0_attn_Wimp': _L0_attn_in['Wimp'], 'L0_attn_bimp': _L0_attn_in['bimp'], 'L0_attn_Walpha': _L0_attn_in['Walpha'], 'L0_attn_balpha': _L0_attn_in['balpha'], 'L0_attn_spike_threshold': _L0_attn_in['spike_threshold'], 'L0_attn_log_k': _L0_attn_in['log_k'], 'L0_attn_qk_scale': _L0_attn_in['qk_scale'], 'L0_ffn_Wr': _L0_ffn_in['Wr'], 'L0_ffn_W1': _L0_ffn_in['W1'], 'L0_ffn_b1': _L0_ffn_in['b1'], 'L0_ffn_Wo': _L0_ffn_in['Wo'], 'L0_ffn_bo': _L0_ffn_in['bo'], 'L0_ffn_gamma': _L0_ffn_in['gamma'], 'L0_ffn_beta': _L0_ffn_in['beta']}
    _x0 = _d['L0_attn_x']
    _d['L0_attn_x'] = jax.random.normal(jax.random.fold_in(jax.random.key(seed), 1), (8, 512, 256), dtype=_x0.dtype)
    del _x0
    return _d

def reference(L0_attn_x, L0_attn_Wqkv, L0_attn_bqkv, L0_attn_Wout, L0_attn_bout, L0_attn_Wimp, L0_attn_bimp, L0_attn_Walpha, L0_attn_balpha, L0_attn_spike_threshold, L0_attn_log_k, L0_attn_qk_scale, L0_ffn_Wr, L0_ffn_W1, L0_ffn_b1, L0_ffn_Wo, L0_ffn_bo, L0_ffn_gamma, L0_ffn_beta):

    def _L0_attn_ref(x, Wqkv, bqkv, Wout, bout, Wimp, bimp, Walpha, balpha, spike_threshold, log_k, qk_scale):
        import math
        import jax, jax.numpy as jnp
        import numpy as np

        def _expmap0(u):
            u0 = u[..., :1]
            us = u[..., 1:]
            mink = -u0 * u0 + jnp.sum(us * us, axis=-1, keepdims=True)
            nomin = jnp.sqrt(jnp.maximum(mink, 1e-08))
            r = jnp.sinh(nomin) * u / nomin
            space = r[..., 1:]
            time = jnp.sqrt(1.0 + jnp.sum(space * space, axis=-1, keepdims=True))
            return jnp.concatenate([time, space], axis=-1)
        B, T, C = x.shape
        H = log_k.shape[0]
        D = C // H
        importance = jax.nn.sigmoid(x @ Wimp.T + bimp)
        spikes = (importance > spike_threshold).astype(x.dtype)
        spike_mask = spikes.reshape(B, 1, T, 1)
        alpha = jax.nn.sigmoid(x @ Walpha.T + balpha)
        alpha = jnp.transpose(alpha, (0, 2, 1))[..., None]
        qkv = (x @ Wqkv.T + bqkv).reshape(B, T, 3, H, D)
        q = jnp.transpose(qkv[:, :, 0], (0, 2, 1, 3))
        k = jnp.transpose(qkv[:, :, 1], (0, 2, 1, 3))
        v = jnp.transpose(qkv[:, :, 2], (0, 2, 1, 3))
        scores_euclid = jnp.einsum('bhtd,bhsd->bhts', q, k) / math.sqrt(D)
        safe_scale = jax.nn.sigmoid(qk_scale) * 1.5
        qn = q / jnp.maximum(jnp.linalg.norm(q, axis=-1, keepdims=True), 1e-12) * safe_scale
        kn = k / jnp.maximum(jnp.linalg.norm(k, axis=-1, keepdims=True), 1e-12) * safe_scale
        q_hyp = _expmap0(qn)
        k_hyp = _expmap0(kn)
        inner = -jnp.einsum('bhti,bhsi->bhts', q_hyp[..., :1], k_hyp[..., :1]) + jnp.einsum('bhtd,bhsd->bhts', q_hyp[..., 1:], k_hyp[..., 1:])
        curv_k = (jax.nn.softplus(log_k) + 1e-06).reshape(1, H, 1, 1)
        mdot = jnp.maximum(-inner, 1.0 + 1e-06)
        dist = jnp.arccosh(mdot)
        scores_hyper = -(dist * dist) / curv_k
        scores = (1.0 - alpha) * scores_euclid + alpha * scores_hyper
        causal = jnp.tril(jnp.ones((T, T), bool))
        scores = jnp.where(causal[None, None], scores, -jnp.inf)
        attn = jax.nn.softmax(scores, axis=-1) * spike_mask
        y = jnp.einsum('bhts,bhsd->bhtd', attn, v)
        y = jnp.transpose(y, (0, 2, 1, 3)).reshape(B, T, C)
        return y @ Wout.T + bout

    def _L0_ffn_ref(hidden_states, Wr, W1, b1, Wo, bo, gamma, beta):
        import jax, jax.numpy as jnp
        import numpy as np
        LN_EPS = 1e-12
        B, S, H = hidden_states.shape
        E = Wr.shape[0]
        x = hidden_states.reshape(-1, H)
        router_logits = x @ Wr.T
        expert_idx = jnp.argmax(jax.nn.softmax(router_logits, axis=-1), axis=-1)
        inter = jnp.zeros((x.shape[0], W1.shape[2]), dtype=x.dtype)
        for e in range(E):
            mask = (expert_idx == e)[:, None].astype(x.dtype)
            inter = inter + mask * jax.nn.gelu(x @ W1[e] + b1[e], approximate=False)
        y = inter @ Wo + bo + x
        mu = jnp.mean(y, axis=-1, keepdims=True)
        var = jnp.mean(jnp.square(y - mu), axis=-1, keepdims=True)
        out = (y - mu) * jax.lax.rsqrt(var + LN_EPS) * gamma + beta
        return out.reshape(B, S, H)
    x = L0_attn_x
    x = x + _layernorm(_L0_attn_ref(_layernorm(x, axis=-1), L0_attn_Wqkv, L0_attn_bqkv, L0_attn_Wout, L0_attn_bout, L0_attn_Wimp, L0_attn_bimp, L0_attn_Walpha, L0_attn_balpha, L0_attn_spike_threshold, L0_attn_log_k, L0_attn_qk_scale), axis=-1)
    x = x + _layernorm(_L0_ffn_ref(_layernorm(x, axis=-1), L0_ffn_Wr, L0_ffn_W1, L0_ffn_b1, L0_ffn_Wo, L0_ffn_bo, L0_ffn_gamma, L0_ffn_beta), axis=-1)
    return x

_drawn_inputs = setup_inputs


def setup_inputs(seed=0):
    import zlib

    import numpy as np

    out = dict(_drawn_inputs(seed))
    spreads = {'L0_attn_bqkv': (0.0, 0.1),
     'L0_attn_bout': (0.0, 0.1),
     'L0_attn_balpha': (0.0, 0.8),
     'L0_attn_log_k': (0.5400000214576721, 0.6),
     'L0_ffn_gamma': (1.0, 0.2),
     'L0_ffn_beta': (0.0, 0.1)}
    factors = {'L0_attn_Walpha': 8.0, 'L0_ffn_b1': 8.0, 'L0_ffn_bo': 7.33}
    for name, (base, spread) in spreads.items():
        noise = np.random.default_rng([zlib.crc32(name.encode()), seed]).standard_normal(out[name].shape)
        drawn = base * np.exp(spread * noise) if base else spread * noise
        out[name] = jnp.asarray(drawn.astype(out[name].dtype))
    for name, factor in factors.items():
        out[name] = (out[name] * factor).astype(out[name].dtype)
    return out
```

```python
import numpy as np
import concourse.bass as bass
from concourse import mybir
from contextlib import ExitStack

F32 = mybir.dt.float32
BF16 = mybir.dt.bfloat16
I32 = mybir.dt.int32
U32 = mybir.dt.uint32
ALU = mybir.AluOpType
ACT = mybir.ActivationFunctionType
AXX = mybir.AxisListType.X

P = 128
B, T, C = 8, 512, 256
H, D = 16, 16
E, FF = 8, 1024
NT = T // P
CC = C // P
FC = FF // P
TOK = B * T
TILES = TOK // P
HG = 4
G = H // HG
QKV = 3 * C
COLS = QKV + H + 1
NQK = 2 * H
SLOTS = TOK // P + E - 1
PER_ITER = 8
ITERS = -(-SLOTS // PER_ITER)
BLOCKS = ITERS * PER_ITER
ROW = C + 1
MASKED = -1e30

FA = 2.5069359320797613
FS = 0.02068334648608328
FB = -2.952890362403119
FC0 = 17.482113414249277
FSCALE = 0.42046220252761046
YMIN = float(np.log1p(0.5e-6))
SINH = [1.0 / 6, 1.0 / 120, 1.0 / 5040, 1.0 / 362880, 1.0 / 39916800, 1.0 / 6227020800]


def inverse_sqrt(nc, link, out, v, t):
    link(nc.vector.tensor_scalar(t.bitcast(I32), v.bitcast(I32), 1, None, ALU.logical_shift_right))
    link(nc.vector.tensor_scalar(out.bitcast(I32), t.bitcast(I32), -1.0, float(0x5F3759DF), ALU.mult, ALU.add))
    for _ in range(3):
        link(nc.vector.scalar_tensor_tensor(out=t, in0=v, scalar=-0.5, in1=out, op0=ALU.mult, op1=ALU.mult))
        link(nc.vector.tensor_tensor(t, t, out, ALU.mult))
        link(nc.vector.scalar_tensor_tensor(out=out, in0=t, scalar=1.5, in1=out, op0=ALU.add, op1=ALU.mult))


def units_of_group():
    out = []
    for h in (0, 2):
        for k in (h, h + 1):
            out.append([(k, 0, 0, P), (k, 2, P, 3 * P)])
            out.append([(k, 3, 0, 4 * P)])
        out.append([(h, 1, 0, 2 * P), (h + 1, 1, 2 * P, 2 * P)])
    return out


UNITS = [(g, u) for g in range(G) for u in units_of_group()]
UG = len(UNITS) // G
NU = len(UNITS)


def sandwich_kernel(nc, x, w_all, b_all, wout_t, bout, thr, log_k, qk_scale, wr_t, w1, b1, wo, bo, gamma, beta, out):
    ctx = ExitStack()
    with ctx:
        def sb(name, shape, dt=F32):
            return ctx.enter_context(nc.sbuf_tensor(name, shape, dt))

        sems = {}

        def sem(name):
            s = ctx.enter_context(nc.semaphore(name))
            sems[name] = s
            return s

        def clear_all():
            ids = sorted(s.num for s in sems.values())
            assert ids == list(range(ids[0], ids[0] + len(ids)))
            nc.all_engine_barrier(sems_to_clear=range(ids[0], ids[-1] + 1))

        PSH = ctx.enter_context(nc.psum_tensor("banks", [P, 8 * 512], F32))
        bank = [PSH[:, 512 * i:512 * (i + 1)] for i in range(8)]
        MB, EB, PTB = (0, 1), (2, 3), (4, 5)
        BA, BB = 6, 7

        ident = sb("ident", [P, P])
        ident_bf = sb("ident_bf", [P, P], BF16)
        mask_bf = sb("mask_bf", [P, P], BF16)
        ones = sb("ones", [P, P])
        lower = sb("lower", [P, P])
        wall = sb("wall", [P, CC, COLS])
        ball = sb("ball", [P, COLS])
        woutT = sb("woutT", [P, CC, C])
        boutB = sb("boutB", [P, C])
        wrT = sb("wrT", [P, CC, E])
        thrB = sb("thrB", [P, 1])
        logk = sb("logk", [P, H])
        lk2 = sb("lk2", [P, H])
        gcoef = sb("gcoef", [P, H])
        qks = sb("qks", [P, 1])
        safe = sb("safe", [P, 1])
        fa_c = sb("fa_c", [P, 1])
        fb_c = sb("fb_c", [P, 1])
        iota_i = sb("iota_i", [P, 64], I32)
        iota_e = sb("iota_e", [P, E])
        iota_k = sb("iota_k", [P, BLOCKS])

        xg = sb("xg", [P, TILES, ROW])
        eidx = sb("eidx", [P, TILES])

        xs_d = nc.dram_tensor("xs_scratch", (BLOCKS * P, ROW), F32, kind="Internal").ap()

        s_sent = ctx.enter_context(nc.semaphore("rows_sent"))
        s_out = [ctx.enter_context(nc.semaphore(f"rows_out_{i}")) for i in range(2)]

        s_w = sem("weights_loaded")
        s_pool0 = sem("pool_constants")
        s_act = sem("act_chain")
        s_dve = sem("dve_chain")
        s_pool = sem("pool_chain")
        s_fill = sem("scratch_filled")
        s_x = sem("x_loaded")
        s_xn = sem("x_normalised")
        s_xT = sem("x_transposed")
        s_xnT = sem("xT_copied")
        s_proj = sem("projected")
        s_qkv = sem("qkv_biased")
        s_sq = sem("squares_ready")
        s_ez = sem("gate_exp_ready")
        s_stats = sem("ratios_ready")
        s_tok = sem("operands_built")
        s_v = sem("values_built")
        s_tokT = sem("operands_transposed")
        s_evac = sem("operands_copied")
        s_m = sem("m_ready")
        s_e = sem("e_ready")
        s_ln = sem("y_ready")
        s_yc = sem("y_clamped")
        s_a = sem("square1_ready")
        s_b = sem("square2_ready")
        s_u = sem("u_ready")
        s_f = sem("f_ready")
        s_comb = sem("scores_ready")
        s_nm = sem("max_ready")
        s_p = sem("probs_ready")
        s_pt = sem("probs_transposed")
        s_ptc = sem("probsT_copied")
        s_pv = sem("pv_done")
        s_ov = sem("pv_copied")
        s_ovT = sem("pv_transposed")
        s_ytok = sem("heads_normalised")
        s_yT = sem("heads_transposed")
        s_yTc = sem("headsT_copied")
        s_o = sem("attention_projected")
        s_x1 = sem("x1_ready")
        s_x1c = sem("x1_kept")
        s_h = sem("h_normalised")
        s_hT = sem("h_transposed")
        s_hTc = sem("hT_copied")
        s_lg = sem("router_logits_ready")
        s_rank = sem("ranks_ready")
        s_oh = sem("onehot_ready")
        s_pos = sem("slots_ready")
        s_rows = [sem(f"rows_loaded_{i}") for i in range(2)]
        s_w1 = [sem(f"expert_loaded_{i}") for i in range(2)]
        s_eh = sem("expert_h_ready")
        s_ehT = sem("expert_h_transposed")
        s_ehTc = sem("expert_hT_copied")
        s_up = sem("expert_up_ready")
        s_gelu = sem("gelu_ready")
        s_down = sem("expert_down_ready")
        s_res = sem("expert_rows_ready")
        s_sum = sem("down_read")

        fill_ctx = ExitStack()
        fill = fill_ctx.enter_context(nc.sbuf_tensor("fill", [P, ROW], F32))
        with nc.Block() as block:
            @block.sync
            def _(sp):
                for c in range(CC):
                    sp.dma_start(wall[:, c, :], w_all[c * P:(c + 1) * P, :]).then_inc(s_w, 16)
                    sp.dma_start(woutT[:, c, :], wout_t[c * P:(c + 1) * P, :]).then_inc(s_w, 16)
                    sp.dma_start(wrT[:, c, :], wr_t[c * P:(c + 1) * P, :]).then_inc(s_w, 16)
                sp.dma_start(ball[:, :], b_all.partition_broadcast(P)).then_inc(s_w, 16)
                sp.dma_start(boutB[:, :], bout.partition_broadcast(P)).then_inc(s_w, 16)
                sp.dma_start(thrB[:, :], thr.partition_broadcast(P)).then_inc(s_w, 16)
                sp.dma_start(logk[:, :], log_k.partition_broadcast(P)).then_inc(s_w, 16)
                sp.dma_start(qks[:, :], qk_scale.partition_broadcast(P)).then_inc(s_w, 16)
                sp.wait_ge(s_w, 16 * (3 * CC + 5))
                sp.wait_ge(s_pool0, 1)
                for k in range(BLOCKS):
                    sp.dma_start(xs_d[k * P:(k + 1) * P, :], fill[:, :]).then_inc(s_fill, 16)
                sp.wait_ge(s_fill, 16 * BLOCKS)

            @block.gpsimd
            def _(pool):
                n = [0]

                def link(ins):
                    n[0] += 1
                    ins.then_inc(s_pool, 1)
                    pool.wait_ge(s_pool, n[0])

                nc.gpsimd.memset(fill[:, 0:C], 0.0)
                nc.gpsimd.memset(fill[:, C:ROW].bitcast(I32), TOK).then_inc(s_pool0, 1)
                nc.gpsimd.memset(ones[:, :], 1.0)
                nc.gpsimd.memset(fa_c[:, :], FA)
                nc.gpsimd.memset(fb_c[:, :], FB)
                nc.gpsimd.memset(ident[:, :], 0.0)
                nc.gpsimd.memset(ident_bf[:, :], 0.0)
                link(nc.gpsimd.memset(mask_bf[:, :], 0.0))
                nc.gpsimd.affine_select(out=ident[:, :], in_=ident[:, :], compare_op=ALU.not_equal, fill=1.0,
                                        base=0, pattern=[[-1, P]], channel_multiplier=1)
                nc.gpsimd.affine_select(out=ident_bf[:, :], in_=ident_bf[:, :], compare_op=ALU.not_equal, fill=1.0,
                                        base=0, pattern=[[-1, P]], channel_multiplier=1)
                nc.gpsimd.affine_select(out=mask_bf[:, :], in_=mask_bf[:, :], compare_op=ALU.is_ge, fill=MASKED,
                                        base=0, pattern=[[-1, P]], channel_multiplier=1)
                link(nc.gpsimd.affine_select(out=lower[:, :], in_=ones[:, :], compare_op=ALU.is_gt, fill=0.0,
                                             base=0, pattern=[[1, P]], channel_multiplier=-1))
                link(nc.gpsimd.iota(xg[:, :, C:ROW].bitcast(I32), pattern=[[P, TILES], [1, 1]], base=0,
                                    channel_multiplier=1))
                link(nc.gpsimd.iota(iota_i[:, 0:BLOCKS], pattern=[[1, BLOCKS]], base=0, channel_multiplier=0))
                nc.gpsimd.tensor_copy(iota_k[:, :], iota_i[:, 0:BLOCKS])
                link(nc.gpsimd.tensor_copy(iota_e[:, :], iota_i[:, 0:E]))

            @block.scalar
            def _(act):
                nc.scalar.preload_act_table_set("natural_log_exp_and_others")
                act.wait_ge(s_w, 16 * (3 * CC + 5))
                nc.scalar.activation(safe[:, :], qks[:, :], ACT.Exp, scale=-1.0).then_inc(s_act, 1)
                act.wait_ge(s_dve, 1)
                nc.scalar.activation(lk2[:, :], gcoef[:, :], ACT.Exp, scale=-1.0).then_inc(s_act, 1)
                act.wait_ge(s_act, 2)
                nc.scalar.activation(gcoef[:, :], lk2[:, :], ACT.Ln, bias=1.0).then_inc(s_act, 1)

            @block.vector
            def _(dve):
                n = [0]

                def link(ins):
                    n[0] += 1
                    ins.then_inc(s_dve, 1)
                    dve.wait_ge(s_dve, n[0])

                dve.wait_ge(s_w, 16 * (3 * CC + 5))
                link(nc.vector.scalar_tensor_tensor(out=gcoef[:, :], in0=logk[:, :], scalar=-1.0, in1=logk[:, :],
                                                    op0=ALU.mult, op1=ALU.max))
                dve.wait_ge(s_act, 1)
                link(nc.vector.tensor_scalar(safe[:, :], safe[:, :], 1.0, None, ALU.add))
                link(nc.vector.reciprocal(safe[:, :], safe[:, :]))
                link(nc.vector.tensor_scalar(safe[:, :], safe[:, :], 1.5, None, ALU.mult))
                dve.wait_ge(s_act, 3)
                link(nc.vector.scalar_tensor_tensor(out=lk2[:, :], in0=logk[:, :], scalar=0.0, in1=gcoef[:, :],
                                                    op0=ALU.max, op1=ALU.add))
                link(nc.vector.tensor_scalar(lk2[:, :], lk2[:, :], 1e-6, None, ALU.add))
                link(nc.vector.reciprocal(lk2[:, :], lk2[:, :]))
                link(nc.vector.tensor_scalar(gcoef[:, :], lk2[:, :], -FSCALE, None, ALU.mult))
        clear_all()
        fill_ctx.close()

        actx = ExitStack()

        def ab(name, shape, dt=F32):
            return actx.enter_context(nc.sbuf_tensor(name, shape, dt))

        x_sb = ab("x_sb", [P, NT, C])
        xn = ab("xn", [P, NT, C])
        xnT = ab("xnT", [P, CC, T])
        st6 = ab("st6", [P, NT, 6])
        mv = ab("mv", [P, NT, 2])
        rstd = ab("rstd", [P, NT])
        vare = ab("vare", [P, NT])
        rtmp = ab("rtmp", [P, NT])
        qkv = ab("qkv", [P, NT, COLS])
        sqb = ab("sqb", [P, NT, NQK, D])
        ez = ab("ez", [P, NT, H + 1])
        spike = ab("spike", [P, NT])
        ga = ab("ga", [P, NT, H])
        be = ab("be", [P, NT, H])
        small = [ab(f"small{i}", [P, NT, NQK]) for i in range(8)]
        ratio = ab("ratio", [P, NT, NQK])
        time_ = ab("time_", [P, NT, NQK])
        tokQ = ab("tokQ", [P, NT, HG, 2 * D])
        tokE = ab("tokE", [P, NT, HG, 2 * D])
        tokM = ab("tokM", [P, NT, HG, 2 * D])
        vaug = [ab(f"vaug{i}", [P, NT, HG, 2 * D]) for i in range(2)]
        Qz = [ab(f"Qz{i}", [P, HG, T]) for i in range(2)]
        KE = [ab(f"KE{i}", [P, T]) for i in range(2)]
        KM = [ab(f"KM{i}", [P, T]) for i in range(2)]
        yR = [ab(f"yR{i}", [P, 512]) for i in range(3)]
        ycR = [ab(f"ycR{i}", [P, 512]) for i in range(3)]
        aR = [ab(f"aR{i}", [P, 512]) for i in range(2)]
        wR = [ab(f"wR{i}", [P, 512]) for i in range(2)]
        uR = [ab(f"uR{i}", [P, 512]) for i in range(2)]
        fR = [ab(f"fR{i}", [P, 512]) for i in range(2)]
        sR = [ab(f"sR{i}", [P, 512]) for i in range(3)]
        pR = [ab(f"pR{i}", [P, 512]) for i in range(3)]
        nm = ab("nm", [P, 4, 2])
        PT = ab("PT", [P, HG, NT, NT, P])
        ov = ab("ov", [P, T])
        rs = ab("rs", [P, NT, HG])
        ytok = ab("ytok", [P, NT, C])
        ob = ab("ob", [P, NT, C])
        lgs = ab("lgs", [P, NT, E])
        mx8 = ab("mx8", [P, NT, 8])
        ix8 = ab("ix8", [P, NT, 8], U32)

        with nc.Block() as block:
            @block.vector
            def _(dve):
                for t in (tokE, tokM):
                    nc.vector.memset(t[:, :, :, :], 0.0)
                for i in range(2):
                    nc.vector.memset(vaug[i][:, :, :, :], 0.0).then_inc(s_dve, 1)
                    nc.vector.memset(Qz[i][:, :, :], 0.0)
                dve.wait_ge(s_dve, 2)
                for i in range(2):
                    nc.vector.memset(vaug[i][:, :, :, D:D + 1], 1.0)
        clear_all()

        x_v = x.rearrange("b (t p) c -> b p t c", p=P)

        def bc(ap, shape):
            return ap.broadcast_to(shape)

        with nc.Fori(0, B) as b:
            with nc.Block() as block:
                @block.sync
                def _(sp):
                    sp.dma_start(x_sb[:, :, :], x_v[bass.ds(b, 1)].rearrange("o p t c -> p (o t) c")).then_inc(s_x, 16)

                @block.vector
                def _(dve):
                    n = [0]

                    def link(ins):
                        n[0] += 1
                        ins.then_inc(s_dve, 1)
                        dve.wait_ge(s_dve, n[0])

                    def layer_norm_stats(src, eps):
                        for j in range(NT):
                            last = nc.vector.bn_stats(st6[:, j, :], src[:, j, :])
                        link(last)
                        for j in range(NT):
                            last = nc.vector.bn_aggr(mv[:, j, :], st6[:, j, :])
                        link(last)
                        link(nc.vector.tensor_scalar(vare[:, :], mv[:, :, 1], eps, None, ALU.add))
                        inverse_sqrt(nc, link, rstd[:, :], vare[:, :], rtmp[:, :])

                    def normalise(dst, src, signal):
                        for j in range(NT):
                            nc.vector.tensor_scalar(dst[:, j, :], src[:, j, :], mv[:, j, 0:1], rstd[:, j:j + 1],
                                                    ALU.subtract, ALU.mult).then_inc(signal, 1)

                    dve.wait_ge(s_x, 16)
                    layer_norm_stats(x_sb, 1e-5)
                    normalise(xn, x_sb, s_xn)
                    for j in range(NT):
                        dve.wait_ge(s_proj, j + 1)
                        nc.vector.tensor_tensor(qkv[:, j, :], PSH[:, 1024 * j:1024 * j + COLS], ball[:, :],
                                                ALU.add).then_inc(s_qkv, 1)
                    dve.wait_ge(s_ez, 1)
                    link(nc.vector.tensor_scalar(ez[:, :, :], ez[:, :, :], 1.0, None, ALU.add))
                    link(nc.vector.reciprocal(ez[:, :, :], ez[:, :, :]))
                    nc.vector.tensor_scalar(spike[:, :], ez[:, :, H], thrB[:, 0:1], None, ALU.is_gt)
                    nc.vector.tensor_tensor(ga[:, :, :], ez[:, :, 0:H],
                                            bc(gcoef[:, :].unsqueeze(1), [P, NT, H]), ALU.mult)
                    link(nc.vector.tensor_scalar(be[:, :, :], ez[:, :, 0:H], -0.25, 0.25, ALU.mult, ALU.add))
                    ss, inv, i2, z, r, sp2, t2, q0 = [s[:, :, :] for s in small]
                    q0 = sqb[:, :, :, 0]
                    dve.wait_ge(s_sq, 1)
                    link(nc.vector.reduce_sum(ss, sqb[:, :, :, :], AXX))
                    nc.vector.tensor_scalar(t2, ss, 1e-24, None, ALU.max)
                    nc.vector.tensor_tensor(sp2, ss, q0, ALU.subtract)
                    link(nc.vector.scalar_tensor_tensor(out=z, in0=q0, scalar=-2.0, in1=ss, op0=ALU.mult, op1=ALU.add))
                    inverse_sqrt(nc, link, inv, t2, i2)
                    link(nc.vector.tensor_scalar(inv, inv, safe[:, 0:1], None, ALU.mult))
                    link(nc.vector.tensor_tensor(i2, inv, inv, ALU.mult))
                    link(nc.vector.tensor_tensor(z, z, i2, ALU.mult))
                    link(nc.vector.tensor_scalar(z, z, 1e-8, None, ALU.max))
                    link(nc.vector.tensor_scalar(r, z, SINH[-1], None, ALU.mult))
                    for c in SINH[-2::-1]:
                        link(nc.vector.scalar_tensor_tensor(out=r, in0=r, scalar=c, in1=z, op0=ALU.add, op1=ALU.mult))
                    link(nc.vector.scalar_tensor_tensor(out=r, in0=r, scalar=1.0, in1=inv, op0=ALU.add, op1=ALU.mult))
                    link(nc.vector.tensor_tensor(t2, r, r, ALU.mult))
                    nc.vector.tensor_copy(ratio[:, :, 0:H], r[:, :, 0:H])
                    nc.vector.tensor_scalar(ratio[:, :, H:NQK], r[:, :, H:NQK], -1.0, None, ALU.mult)
                    link(nc.vector.tensor_tensor(t2, t2, sp2, ALU.mult))
                    link(nc.vector.tensor_scalar(t2, t2, 1.0, None, ALU.add))
                    inverse_sqrt(nc, link, i2, t2, z)
                    nc.vector.tensor_tensor(time_[:, :, :], t2, i2, ALU.mult).then_inc(s_stats, 1)

                    def distance(k):
                        dve.wait_ge(s_u, k + 1)
                        if k >= 2:
                            dve.wait_ge(s_comb, k - 1)
                        nc.vector.scalar_tensor_tensor(out=fR[k % 2][:, :], in0=uR[k % 2][:, :], scalar=FC0,
                                                       in1=ycR[k % 3][:, :], op0=ALU.add, op1=ALU.mult).then_inc(s_f, 1)

                    def scores(k):
                        g, unit = UNITS[k]
                        dve.wait_ge(s_f, k + 1)
                        dve.wait_ge(s_e, k + 1)
                        if k >= 3:
                            dve.wait_ge(s_p, k - 2)
                        for h, t, off, w in unit:
                            last = nc.vector.scalar_tensor_tensor(
                                out=sR[k % 3][:, off:off + w], in0=fR[k % 2][:, off:off + w],
                                scalar=ga[:, t, g * HG + h:g * HG + h + 1], in1=bank[EB[k % 2]][:, off:off + w],
                                op0=ALU.mult, op1=ALU.add)
                        last.then_inc(s_comb, 1)

                    def maxima(k):
                        dve.wait_ge(s_comb, k + 1)
                        for i, (h, t, off, w) in enumerate(UNITS[k][1]):
                            last = nc.vector.tensor_reduce(nm[:, k % 4, i:i + 1], sR[k % 3][:, off:off + w], AXX,
                                                           ALU.max, negate=True)
                        last.then_inc(s_nm, 1)

                    def keep_probsT(k):
                        g, unit = UNITS[k]
                        dve.wait_ge(s_pt, k + 1)
                        if k % UG == 0 and g >= 1:
                            dve.wait_ge(s_pv, g)
                        src = bank[PTB[k % 2]]
                        if len(unit) == 2 and unit[0][1] == 1:
                            h = unit[0][0]
                            last = nc.vector.tensor_copy(PT[:, h:h + 2, 0:2, 1, :],
                                                         src.rearrange("p (h j q) -> p h j q", h=2, j=2))
                        else:
                            for h, t, off, w in unit:
                                last = nc.vector.tensor_copy(PT[:, h, 0:t + 1, t, :],
                                                             src[:, off:off + w].rearrange("p (j q) -> p j q", q=P))
                        last.then_inc(s_ptc, 1)

                    def heads(g):
                        dve.wait_ge(s_ovT, g + 1)
                        v = bank[BA].rearrange("p (t h d) -> p t h d", t=NT, h=HG)
                        link(nc.vector.reciprocal(rs[:, :, :], v[:, :, :, D]))
                        link(nc.vector.tensor_tensor(rs[:, :, :], rs[:, :, :],
                                                     bc(spike[:, :].unsqueeze(2), [P, NT, HG]), ALU.mult))
                        dst = ytok[:, :, g * HG * D:(g + 1) * HG * D].rearrange("p t (h d) -> p t h d", h=HG)
                        nc.vector.tensor_tensor(dst, v[:, :, :, 0:D], bc(rs[:, :, :].unsqueeze(3), [P, NT, HG, D]),
                                                ALU.mult).then_inc(s_ytok, 1)

                    for k in range(NU + 7):
                        if 1 <= k <= NU:
                            distance(k - 1)
                        if 5 <= k < NU + 5:
                            keep_probsT(k - 5)
                        if 1 <= k <= NU:
                            scores(k - 1)
                            maxima(k - 1)
                        if k >= UG + 6 and (k - 6) % UG == 0:
                            heads((k - 6) // UG - 1)

                    dve.wait_ge(s_o, NT)
                    link(nc.vector.tensor_tensor(ob[:, :, :], PSH[:, 1024:2048].rearrange("p (t c) -> p t c", t=NT),
                                                 bc(boutB[:, :].unsqueeze(1), [P, NT, C]), ALU.add))
                    layer_norm_stats(ob, 1e-5)
                    for j in range(NT):
                        last = nc.vector.tensor_scalar(ob[:, j, :], ob[:, j, :], mv[:, j, 0:1], rstd[:, j:j + 1],
                                                       ALU.subtract, ALU.mult)
                    link(last)
                    link(nc.vector.tensor_tensor(x_sb[:, :, :], x_sb[:, :, :], ob[:, :, :], ALU.add))
                    nc.vector.tensor_copy(rs[:, :, 0], mv[:, :, 0]).then_inc(s_x1, 1)
                    layer_norm_stats(x_sb, 1e-5)
                    normalise(xn, x_sb, s_h)
                    dve.wait_ge(s_lg, 1)
                    link(nc.vector.tensor_copy(lgs[:, :, :], bank[BA][:, 0:NT * E].rearrange("p (t e) -> p t e", t=NT)))
                    for j in range(NT):
                        last = nc.vector.max(mx8[:, j, :], lgs[:, j, :])
                    link(last)
                    for j in range(NT):
                        last = nc.vector.max_index(ix8[:, j, :], mx8[:, j, :], lgs[:, j, :])
                    link(last)
                    nc.vector.tensor_copy(eidx[:, bass.ds(b * NT, NT)], ix8[:, :, 0])

                @block.scalar
                def _(act):
                    for c in range(CC):
                        act.wait_ge(s_xT, c + 1)
                        nc.scalar.copy(xnT[:, c, :], bank[6 + c]).then_inc(s_xnT, 1)
                    act.wait_ge(s_qkv, NT)
                    nc.scalar.activation(ez[:, :, :], qkv[:, :, QKV:COLS], ACT.Exp, scale=-1.0).then_inc(s_ez, 1)
                    nc.scalar.activation(sqb[:, :, :, :].rearrange("p t n d -> p t (n d)"), qkv[:, :, 0:2 * C],
                                         ACT.Square).then_inc(s_sq, 1)

                    def copy_operands_qe(g):
                        i = g % 2
                        if g >= 2:
                            act.wait_ge(s_e, UG * (g - 1))
                        act.wait_ge(s_tokT, 3 * g + 1)
                        for h in range(HG):
                            rows = slice(2 * D * h, 2 * D * (h + 1))
                            last = nc.scalar.copy(Qz[i][rows, h, :], bank[BA][rows, :])
                        last.then_inc(s_evac, 1)
                        act.wait_ge(s_tokT, 3 * g + 2)
                        nc.scalar.copy(KE[i][:, :], bank[BB]).then_inc(s_evac, 1)

                    def copy_operands_m(g):
                        act.wait_ge(s_tokT, 3 * g + 3)
                        nc.scalar.copy(KM[g % 2][:, :], bank[BA]).then_inc(s_evac, 1)

                    def log(k):
                        act.wait_ge(s_m, k + 1)
                        if k >= 3:
                            act.wait_ge(s_yc, k - 2)
                        nc.scalar.activation(yR[k % 3][:, :], bank[MB[k % 2]], ACT.Ln, bias=0.5,
                                             scale=0.5).then_inc(s_ln, 1)

                    def square1(k):
                        act.wait_ge(s_ln, k + 1)
                        if k >= 2:
                            act.wait_ge(s_b, k - 1)
                        nc.scalar.activation(aR[k % 2][:, :], yR[k % 3][:, :], ACT.Square,
                                             bias=fa_c[:, 0:1]).then_inc(s_a, 1)

                    def square2(k):
                        act.wait_ge(s_a, k + 1)
                        if k >= 2:
                            act.wait_ge(s_u, k - 1)
                        nc.scalar.activation(wR[k % 2][:, :], aR[k % 2][:, :], ACT.Square, bias=fb_c[:, 0:1],
                                             scale=FS).then_inc(s_b, 1)

                    def probs(k):
                        act.wait_ge(s_nm, k + 1)
                        if k >= 3:
                            act.wait_ge(s_pt, k - 2)
                        for i, (h, t, off, w) in enumerate(UNITS[k][1]):
                            last = nc.scalar.activation(pR[k % 3][:, off:off + w], sR[k % 3][:, off:off + w], ACT.Exp,
                                                        bias=nm[:, k % 4, i:i + 1])
                        last.then_inc(s_p, 1)

                    def copy_pv(g):
                        act.wait_ge(s_pv, g + 1)
                        if g >= 1:
                            act.wait_ge(s_ovT, g)
                        nc.scalar.copy(ov[:, :], bank[BB]).then_inc(s_ov, 1)

                    copy_operands_qe(0)
                    copy_operands_m(0)
                    for k in range(NU + 7):
                        if k < NU:
                            log(k)
                        if 3 <= k < NU + 3:
                            probs(k - 3)
                        if k < NU:
                            square1(k)
                        if k % UG == 8 and k // UG + 1 < G:
                            copy_operands_qe(k // UG + 1)
                        if k % UG == 9 and k // UG + 1 < G:
                            copy_operands_m(k // UG + 1)
                        if k >= UG + 5 and (k - 5) % UG == 0:
                            copy_pv((k - 5) // UG - 1)
                        if k < NU:
                            square2(k)

                    for c in range(CC):
                        act.wait_ge(s_yT, c + 1)
                        nc.scalar.copy(xnT[:, c, :], bank[c]).then_inc(s_yTc, 1)
                    act.wait_ge(s_x1, 1)
                    nc.scalar.copy(xg[:, bass.ds(b * NT, NT), 0:C], x_sb[:, :, :]).then_inc(s_x1c, 1)
                    for c in range(CC):
                        act.wait_ge(s_hT, c + 1)
                        act.wait_ge(s_o, NT)
                        nc.scalar.copy(xnT[:, c, :], bank[4 + c]).then_inc(s_hTc, 1)

                @block.gpsimd
                def _(pool):
                    def part(base, g):
                        return qkv[:, :, base + g * HG * D:base + (g + 1) * HG * D].rearrange(
                            "p t (h d) -> p t h d", h=HG)

                    def build(g):
                        hs = slice(g * HG, (g + 1) * HG)
                        hk = slice(H + g * HG, H + (g + 1) * HG)

                        q, kk = part(0, g), part(C, g)
                        if g == 0:
                            pool.wait_ge(s_stats, 1)
                        else:
                            pool.wait_ge(s_tokT, 3 * g)
                        S = [P, NT, HG, D]
                        S1 = [P, NT, HG, D - 1]
                        nc.gpsimd.tensor_tensor(tokQ[:, :, :, 0:D], q, bc(be[:, :, hs].unsqueeze(3), S),
                                                ALU.mult).then_inc(s_tok, 1)
                        nc.gpsimd.tensor_tensor(tokQ[:, :, :, D + 1:2 * D], q[:, :, :, 1:D],
                                                bc(ratio[:, :, hs].unsqueeze(3), S1), ALU.mult).then_inc(s_tok, 1)
                        nc.gpsimd.tensor_copy(tokQ[:, :, :, D], time_[:, :, hs]).then_inc(s_tok, 1)
                        nc.gpsimd.tensor_copy(tokE[:, :, :, 0:D], kk).then_inc(s_tok, 1)
                        nc.gpsimd.tensor_tensor(tokM[:, :, :, D + 1:2 * D], kk[:, :, :, 1:D],
                                                bc(ratio[:, :, hk].unsqueeze(3), S1), ALU.mult).then_inc(s_tok, 1)
                        nc.gpsimd.tensor_copy(tokM[:, :, :, D], time_[:, :, hk]).then_inc(s_tok, 1)

                    def build_values(g):
                        if g >= 2:
                            pool.wait_ge(s_pv, g - 1)
                        nc.gpsimd.tensor_copy(vaug[g % 2][:, :, :, 0:D], part(2 * C, g)).then_inc(s_v, 1)

                    def clamp(k):
                        pool.wait_ge(s_ln, k + 1)
                        if k >= 3:
                            pool.wait_ge(s_f, k - 2)
                        nc.gpsimd.tensor_scalar(ycR[k % 3][:, :], yR[k % 3][:, :], 1e30, YMIN, ALU.min,
                                                ALU.max).then_inc(s_yc, 1)

                    def difference(k):
                        pool.wait_ge(s_b, k + 1)
                        pool.wait_ge(s_yc, k + 1)
                        if k >= 2:
                            pool.wait_ge(s_f, k - 1)
                        nc.gpsimd.tensor_tensor(uR[k % 2][:, :], ycR[k % 3][:, :], wR[k % 2][:, :],
                                                ALU.subtract).then_inc(s_u, 1)

                    build(0)
                    build_values(0)
                    for k in range(NU):
                        clamp(k)
                        difference(k)
                        if k % UG == 3 and k // UG + 1 < G:
                            build(k // UG + 1)
                        if k % UG == 7 and k // UG + 1 < G:
                            build_values(k // UG + 1)

                @block.tensor
                def _(pe):
                    pe.wait_ge(s_xn, NT)
                    for c in range(CC):
                        for j in range(NT):
                            last = nc.tensor.transpose(bank[6 + c][:, j * P:(j + 1) * P],
                                                       xn[:, j, c * P:(c + 1) * P], ident[:, :])
                        last.then_inc(s_xT, 1)
                    pe.wait_ge(s_xnT, CC)
                    for j in range(NT):
                        for b0, c0, c1 in ((0, 0, 512), (1, 512, COLS)):
                            for c in range(CC):
                                last = nc.tensor.matmul(bank[2 * j + b0][:, 0:c1 - c0], xnT[:, c, j * P:(j + 1) * P],
                                                        wall[:, c, c0:c1], start=(c == 0), stop=(c == CC - 1))
                        last.then_inc(s_proj, 1)

                    def transpose_into(dst, src):
                        for j in range(NT):
                            last = nc.tensor.transpose(bank[dst][:, j * P:(j + 1) * P],
                                                       src[:, j, :, :].rearrange("p h d -> p (h d)"), ident[:, :])
                        last.then_inc(s_tokT, 1)

                    def transpose_operands_qe(g):
                        pe.wait_ge(s_tok, 6 * (g + 1))
                        if g >= 1:
                            pe.wait_ge(s_evac, 3 * g)
                        if g >= 2:
                            pe.wait_ge(s_ytok, g - 1)
                            pe.wait_ge(s_ov, g - 1)
                        transpose_into(BA, tokQ)
                        transpose_into(BB, tokE)

                    def transpose_operands_m(g):
                        pe.wait_ge(s_evac, 3 * g + 1)
                        transpose_into(BA, tokM)

                    def lorentz(k):
                        g, unit = UNITS[k]
                        if k % UG == 0:
                            pe.wait_ge(s_evac, 3 * (g + 1))
                        if k >= 2:
                            pe.wait_ge(s_ln, k - 1)
                        for h, t, off, w in unit:
                            last = nc.tensor.matmul(bank[MB[k % 2]][:, off:off + w],
                                                    Qz[g % 2][:, h, t * P:(t + 1) * P], KM[g % 2][:, 0:w],
                                                    start=True, stop=True)
                        last.then_inc(s_m, 1)

                    def dots(k):
                        g, unit = UNITS[k]
                        if k >= 2:
                            pe.wait_ge(s_comb, k - 1)
                        for h, t, off, w in unit:
                            dst = bank[EB[k % 2]]
                            nc.tensor.matmul(dst[:, off:off + w], Qz[g % 2][:, h, t * P:(t + 1) * P],
                                             KE[g % 2][:, 0:w], start=True, stop=False)
                            last = nc.tensor.matmul(dst[:, off + w - P:off + w], ident_bf[:, :], mask_bf[:, :],
                                                    start=False, stop=True)
                        last.then_inc(s_e, 1)

                    def transpose_probs(k):
                        pe.wait_ge(s_p, k + 1)
                        if k >= 2:
                            pe.wait_ge(s_ptc, k - 1)
                        for j in range(4):
                            last = nc.tensor.transpose(bank[PTB[k % 2]][:, j * P:(j + 1) * P],
                                                       pR[k % 3][:, j * P:(j + 1) * P], ident[:, :])
                        last.then_inc(s_pt, 1)

                    def values(g):
                        pe.wait_ge(s_v, g + 1)
                        pe.wait_ge(s_ptc, UG * (g + 1))
                        pe.wait_ge(s_evac, 3 * min(g + 2, G))
                        if g >= 1:
                            pe.wait_ge(s_ov, g)
                        for j in range(NT):
                            for h in range(HG):
                                last = nc.tensor.matmul(bank[BB][2 * D * h:2 * D * (h + 1), j * P:T],
                                                        vaug[g % 2][:, j, h, :],
                                                        PT[:, h, j, j:NT, :].rearrange("p t q -> p (t q)"),
                                                        start=(j == 0), stop=(j == NT - 1),
                                                        tile_position=(0, 2 * D * h), skip_group_check=True)
                        last.then_inc(s_pv, 1)

                    def transpose_values(g):
                        pe.wait_ge(s_ov, g + 1)
                        if g >= 1:
                            pe.wait_ge(s_ytok, g)
                        for j in range(NT):
                            last = nc.tensor.transpose(bank[BA][:, j * P:(j + 1) * P], ov[:, j * P:(j + 1) * P],
                                                       ident[:, :])
                        last.then_inc(s_ovT, 1)

                    pe.wait_ge(s_qkv, NT)
                    transpose_operands_qe(0)
                    transpose_operands_m(0)
                    for k in range(NU + 7):
                        if k < NU:
                            lorentz(k)
                        if 1 <= k <= NU:
                            dots(k - 1)
                        if 4 <= k < NU + 4:
                            transpose_probs(k - 4)
                        if k % UG == 7 and k // UG + 1 < G:
                            transpose_operands_qe(k // UG + 1)
                        if k % UG == 8 and k // UG + 1 < G:
                            transpose_operands_m(k // UG + 1)
                        if k >= UG + 5 and (k - 5) % UG == 0:
                            values((k - 5) // UG - 1)
                        if k >= UG + 6 and (k - 6) % UG == 0:
                            transpose_values((k - 6) // UG - 1)

                    pe.wait_ge(s_ytok, G)
                    for c in range(CC):
                        for j in range(NT):
                            last = nc.tensor.transpose(bank[c][:, j * P:(j + 1) * P], ytok[:, j, c * P:(c + 1) * P],
                                                       ident[:, :])
                        last.then_inc(s_yT, 1)
                    pe.wait_ge(s_yTc, CC)
                    for j in range(NT):
                        for c in range(CC):
                            last = nc.tensor.matmul(bank[2 + j // 2][:, (j % 2) * C:(j % 2 + 1) * C],
                                                    xnT[:, c, j * P:(j + 1) * P], woutT[:, c, :],
                                                    start=(c == 0), stop=(c == CC - 1))
                        last.then_inc(s_o, 1)
                    pe.wait_ge(s_h, NT)
                    for c in range(CC):
                        for j in range(NT):
                            last = nc.tensor.transpose(bank[4 + c][:, j * P:(j + 1) * P], xn[:, j, c * P:(c + 1) * P],
                                                       ident[:, :])
                        last.then_inc(s_hT, 1)
                    pe.wait_ge(s_hTc, CC)
                    for j in range(NT):
                        for c in range(CC):
                            last = nc.tensor.matmul(bank[BA][:, j * E:(j + 1) * E], xnT[:, c, j * P:(j + 1) * P],
                                                    wrT[:, c, :], start=(c == 0), stop=(c == CC - 1))
                    last.then_inc(s_lg, 1)
            clear_all()
        actx.close()

        slot_expert = sb("slot_expert", [P, BLOCKS], I32)
        rctx = ExitStack()

        def rb(name, shape, dt=F32):
            return rctx.enter_context(nc.sbuf_tensor(name, shape, dt))

        onehot = rb("onehot", [P, TILES, E])
        tots = rb("tots", [P, TILES, E])
        cum = [rb(f"cum{i}", [P, TILES, E]) for i in range(2)]
        cnt_i = rb("cnt_i", [P, E], I32)
        padded = rb("padded", [P, E])
        ends = [rb(f"ends{i}", [P, E]) for i in range(2)]
        cmp = rb("cmp", [P, BLOCKS, E])
        posf = rb("posf", [P, TILES])
        pos = rb("pos", [P, TILES], I32)
        ebf = rb("ebf", [P, BLOCKS])
        with nc.Block() as block:
            @block.vector
            def _(dve):
                n = [0]

                def link(ins):
                    n[0] += 1
                    ins.then_inc(s_dve, 1)
                    dve.wait_ge(s_dve, n[0])

                nc.vector.tensor_tensor(onehot[:, :, :], bc(eidx[:, :].unsqueeze(2), [P, TILES, E]),
                                        bc(iota_e[:, :].unsqueeze(1), [P, TILES, E]), ALU.is_equal).then_inc(s_oh, 1)
                dve.wait_ge(s_rank, 1)
                tot_ps = bank[1][:, 0:TILES * E].rearrange("p (i e) -> p i e", e=E)
                rank_ps = bank[0][:, 0:TILES * E].rearrange("p (i e) -> p i e", e=E)
                nc.vector.tensor_copy(tots[:, :, :], tot_ps)
                link(nc.vector.tensor_copy(cum[0][:, :, :], tot_ps))
                src, dst, s = 0, 1, 1
                while s < TILES:
                    nc.vector.tensor_copy(cum[dst][:, 0:s, :], cum[src][:, 0:s, :])
                    link(nc.vector.tensor_tensor(cum[dst][:, s:TILES, :], cum[src][:, s:TILES, :],
                                                 cum[src][:, 0:TILES - s, :], ALU.add))
                    src, dst, s = dst, src, 2 * s
                incl = cum[src]
                link(nc.vector.tensor_scalar(padded[:, :], incl[:, TILES - 1, :], float(P - 1), None, ALU.add))
                link(nc.vector.tensor_copy(cnt_i[:, :], padded[:, :]))
                link(nc.vector.tensor_scalar(cnt_i[:, :], cnt_i[:, :], 7, 7, ALU.logical_shift_right,
                                             ALU.logical_shift_left))
                link(nc.vector.tensor_copy(padded[:, :], cnt_i[:, :]))
                link(nc.vector.tensor_copy(ends[0][:, :], padded[:, :]))
                a, z, s = 0, 1, 1
                while s < E:
                    nc.vector.tensor_copy(ends[z][:, 0:s], ends[a][:, 0:s])
                    link(nc.vector.tensor_tensor(ends[z][:, s:E], ends[a][:, s:E], ends[a][:, 0:E - s], ALU.add))
                    a, z, s = z, a, 2 * s
                end = ends[a]
                link(nc.vector.tensor_tensor(incl[:, :, :], incl[:, :, :], tots[:, :, :], ALU.subtract))
                link(nc.vector.tensor_tensor(incl[:, :, :], incl[:, :, :], rank_ps, ALU.add))
                link(nc.vector.tensor_tensor(padded[:, :], end[:, :], padded[:, :], ALU.subtract))
                link(nc.vector.tensor_tensor(incl[:, :, :], incl[:, :, :],
                                             bc(padded[:, :].unsqueeze(1), [P, TILES, E]), ALU.add))
                link(nc.vector.tensor_tensor(incl[:, :, :], incl[:, :, :], onehot[:, :, :], ALU.mult))
                link(nc.vector.reduce_sum(posf[:, :], incl[:, :, :], AXX))
                nc.vector.tensor_copy(pos[:, :], posf[:, :]).then_inc(s_pos, 1)
                link(nc.vector.tensor_scalar(ebf[:, :], iota_k[:, :], float(P), None, ALU.mult))
                link(nc.vector.tensor_tensor(cmp[:, :, :], bc(end[:, :].unsqueeze(1), [P, BLOCKS, E]),
                                             bc(ebf[:, :].unsqueeze(2), [P, BLOCKS, E]), ALU.is_le))
                link(nc.vector.reduce_sum(ebf[:, :], cmp[:, :, :], AXX))
                link(nc.vector.tensor_scalar(ebf[:, :], ebf[:, :], float(E - 1), None, ALU.min))
                link(nc.vector.tensor_copy(slot_expert[:, :], ebf[:, :]))

            @block.tensor
            def _(pe):
                pe.wait_ge(s_oh, 1)
                oh = onehot[:, :, :].rearrange("p i e -> p (i e)")
                nc.tensor.matmul(bank[0][:, 0:TILES * E], lower[:, :], oh, start=True, stop=True)
                nc.tensor.matmul(bank[1][:, 0:TILES * E], ones[:, :], oh, start=True, stop=True).then_inc(s_rank, 1)

            @block.gpsimd
            def _(pool):
                pool.wait_ge(s_pos, 1)
                for i in range(TILES):
                    pool.indirect_dma_start(out=xs_d, out_offset=bass.IndirectOffsetOnAxis(ap=pos[:, i:i + 1], axis=0),
                                            in_=xg[:, i, :], in_offset=None).then_inc(s_sent, 16)
                pool.wait_ge(s_sent, 16 * TILES)
        clear_all()
        rctx.close()

        w1_v = w1.rearrange("e (c p) f -> e p c f", p=P)
        b1_v = b1.rearrange("e (f p) -> e p f", p=P)
        xs_v = xs_d.rearrange("(k p) c -> k p c", p=P)
        out_v = out.rearrange("b t c -> (b t) c")
        woS = sb("woS", [P, FC, C])
        boB = sb("boB", [P, C])
        gaB = sb("gaB", [P, C])
        beB = sb("beB", [P, C])
        R = 2
        rows = [sb(f"rows{i}", [P, ROW]) for i in range(R)]
        w1S = [sb(f"w1S{i}", [P, CC, FF]) for i in range(R)]
        b1S = [sb(f"b1S{i}", [P, FC]) for i in range(R)]
        hn = [sb(f"hn{i}", [P, C]) for i in range(R)]
        hnT = [sb(f"hnT{i}", [P, CC, P]) for i in range(R)]
        hid = [sb(f"hid{i}", [P, FC, P]) for i in range(R)]
        acc = [sb(f"acc{i}", [P, C]) for i in range(R)]
        res = [sb(f"res{i}", [P, C]) for i in range(R)]
        ids = [sb(f"ids{i}", [P, 1], I32) for i in range(R)]
        s1 = [sb(f"s1_{i}", [P, 6]) for i in range(3)]
        m1 = [sb(f"m1_{i}", [P, 2]) for i in range(3)]
        r1 = [sb(f"r1_{i}", [P, 1]) for i in range(3)]
        v1 = [sb(f"v1_{i}", [P, 1]) for i in range(3)]
        t1 = [sb(f"t1_{i}", [P, 1]) for i in range(3)]
        with nc.Block() as block:
            @block.sync
            def _(sp):
                sp.dma_start(woS[:, :, :], wo.rearrange("(f p) c -> p f c", p=P)).then_inc(s_w, 16)
                for dst, src in ((boB, bo), (gaB, gamma), (beB, beta)):
                    sp.dma_start(dst[:, :], src.partition_broadcast(P)).then_inc(s_w, 16)
                sp.wait_ge(s_w, 64)
        clear_all()

        with nc.Fori(0, ITERS) as it:
            with nc.Block() as block:
                @block.sync
                def _(sp):
                    for k in range(PER_ITER):
                        i = k % R
                        if k >= R:
                            sp.wait_ge(s_up, k - R + 1)
                            sp.wait_ge(s_gelu, 2 * (k - R + 1))
                            sp.wait_ge(s_res, k - R + 1)
                        sp.dma_start(rows[i][:, :], xs_v[bass.ds(it * PER_ITER + k, 1)].rearrange("o p c -> p (o c)")
                                     ).then_inc(s_rows[i], 16)
                        e = sp.value_load(slot_expert[0:1, bass.ds(it * PER_ITER + k, 1)], min_val=0, max_val=E - 1)
                        sp.dma_start(w1S[i][:, :, :], w1_v[bass.ds(e, 1)].rearrange("o p c f -> p (o c) f")
                                     ).then_inc(s_w1[i], 16)
                        with nc.allow_non_contiguous_dma("an expert's bias, a column per chunk"):
                            sp.dma_start(b1S[i][:, :], b1_v[bass.ds(e, 1)].rearrange("o p f -> p (o f)")
                                         ).then_inc(s_w1[i], 16)

                @block.vector
                def _(dve):
                    n = [0]

                    def link(ins):
                        n[0] += 1
                        ins.then_inc(s_dve, 1)
                        dve.wait_ge(s_dve, n[0])

                    def stats(i, src, eps):
                        link(nc.vector.bn_stats(s1[i][:, :], src))
                        link(nc.vector.bn_aggr(m1[i][:, :], s1[i][:, :]))
                        link(nc.vector.tensor_scalar(v1[i][:, :], m1[i][:, 1:2], eps, None, ALU.add))
                        inverse_sqrt(nc, link, r1[i][:, :], v1[i][:, :], t1[i][:, :])

                    def before(k):
                        i = k % R
                        dve.wait_ge(s_rows[i], 16 * (k // R + 1))
                        stats(0, rows[i][:, 0:C], 1e-5)
                        nc.vector.tensor_scalar(hn[i][:, :], rows[i][:, 0:C], m1[0][:, 0:1], r1[0][:, 0:1],
                                                ALU.subtract, ALU.mult).then_inc(s_eh, 1)
                        dve.wait_ge(s_ehT, k + 1)
                        if k >= R:
                            dve.wait_ge(s_up, k - R + 1)
                        nc.vector.tensor_copy(hnT[i][:, :, :], bank[6][:, 0:CC * P].rearrange("p (c q) -> p c q", c=CC)
                                              ).then_inc(s_ehTc, 1)
                        dve.wait_ge(s_eh, k + 1)
                        link(nc.vector.tensor_tensor(hn[i][:, :], hn[i][:, :], boB[:, :], ALU.add))

                    def after(k):
                        i = k % R
                        a = acc[i][:, :]
                        dve.wait_ge(s_down, k + 1)
                        nc.vector.tensor_tensor(a, bank[4 + i][:, 0:C], hn[i][:, :], ALU.add).then_inc(s_sum, 1)
                        dve.wait_ge(s_sum, k + 1)
                        stats(1, a, 1e-12)
                        link(nc.vector.tensor_scalar(a, a, m1[1][:, 0:1], r1[1][:, 0:1], ALU.subtract, ALU.mult))
                        link(nc.vector.tensor_tensor(a, a, gaB[:, :], ALU.mult))
                        link(nc.vector.tensor_tensor(a, a, beB[:, :], ALU.add))
                        stats(2, a, 1e-5)
                        if k >= R:
                            dve.wait_ge(s_out[i], it * (16 * PER_ITER // R) + 16 * (k // R))
                        link(nc.vector.tensor_scalar(a, a, m1[2][:, 0:1], r1[2][:, 0:1], ALU.subtract, ALU.mult))
                        nc.vector.tensor_copy(ids[i][:, :], rows[i][:, C:ROW].bitcast(I32))
                        nc.vector.tensor_tensor(res[i][:, :], a, rows[i][:, 0:C], ALU.add).then_inc(s_res, 1)

                    before(0)
                    for k in range(PER_ITER):
                        if k + 1 < PER_ITER:
                            before(k + 1)
                        after(k)

                @block.scalar
                def _(act):
                    for k in range(PER_ITER):
                        i = k % R
                        act.wait_ge(s_w1[i], 32 * (k // R + 1))
                        if k >= R:
                            act.wait_ge(s_down, k - R + 1)
                        for half in range(2):
                            act.wait_ge(s_up, k + 1)
                            for f in range(half * FC // 2, (half + 1) * FC // 2):
                                last = nc.scalar.activation(hid[i][:, f, :],
                                                            PSH[:, 1024 * i + P * f:1024 * i + P * (f + 1)], ACT.Gelu,
                                                            bias=b1S[i][:, f:f + 1])
                            last.then_inc(s_gelu, 1)

                @block.tensor
                def _(pe):
                    def turn(k):
                        pe.wait_ge(s_eh, k + 1)
                        if k >= 1:
                            pe.wait_ge(s_ehTc, k)
                        for c in range(CC):
                            last = nc.tensor.transpose(bank[6][:, c * P:(c + 1) * P], hn[k % R][:, c * P:(c + 1) * P],
                                                       ident[:, :])
                        last.then_inc(s_ehT, 1)

                    def up(k):
                        i = k % R
                        pe.wait_ge(s_ehTc, k + 1)
                        pe.wait_ge(s_w1[i], 32 * (k // R + 1))
                        if k >= R:
                            pe.wait_ge(s_gelu, 2 * (k - R + 1))
                        for f in range(FC):
                            for c in range(CC):
                                last = nc.tensor.matmul(PSH[:, 1024 * i + P * f:1024 * i + P * (f + 1)],
                                                        w1S[i][:, c, f * P:(f + 1) * P], hnT[i][:, c, :],
                                                        start=(c == 0), stop=(c == CC - 1))
                        last.then_inc(s_up, 1)

                    def down(k):
                        i = k % R
                        if k >= R:
                            pe.wait_ge(s_sum, k - R + 1)
                        for f in range(FC):
                            pe.wait_ge(s_gelu, 2 * k + 1 + f // (FC // 2))
                            last = nc.tensor.matmul(bank[4 + i][:, 0:C], hid[i][:, f, :], woS[:, f, :],
                                                    start=(f == 0), stop=(f == FC - 1))
                        last.then_inc(s_down, 1)

                    turn(0)
                    up(0)
                    for k in range(PER_ITER):
                        if k + 1 < PER_ITER:
                            turn(k + 1)
                            up(k + 1)
                        down(k)

                @block.gpsimd
                def _(pool):
                    for k in range(PER_ITER):
                        i = k % R
                        pool.wait_ge(s_res, k + 1)
                        pool.indirect_dma_start(out=out_v,
                                                out_offset=bass.IndirectOffsetOnAxis(ap=ids[i][:, 0:1], axis=0),
                                                in_=res[i][:, :], in_offset=None, bounds_check=TOK - 1,
                                                oob_is_err=False).then_inc(s_out[i], 16)
                    for i in range(R):
                        pool.wait_ge(s_out[i], it * (16 * PER_ITER // R) + 16 * PER_ITER // R)
            clear_all()


def kernel(**inputs):
    import numpy as _np
    import concourse.bacc as _bacc
    from concourse import mybir as _mybir
    from concourse.bass_utils import run_bass_kernel_spmd as _run

    a = {k: _np.asarray(v) for k, v in inputs.items()}
    tr = lambda m: _np.ascontiguousarray(_np.swapaxes(m, -1, -2))
    laid = [
        ("x", a["L0_attn_x"]),
        ("w_all", _np.ascontiguousarray(_np.concatenate(
            [tr(a["L0_attn_Wqkv"]), tr(a["L0_attn_Walpha"]), tr(a["L0_attn_Wimp"])], axis=1))),
        ("b_all", _np.concatenate([a["L0_attn_bqkv"], a["L0_attn_balpha"], a["L0_attn_bimp"]])),
        ("wout_t", tr(a["L0_attn_Wout"])),
        ("bout", a["L0_attn_bout"]),
        ("thr", a["L0_attn_spike_threshold"].reshape(1)),
        ("log_k", a["L0_attn_log_k"]),
        ("qk_scale", a["L0_attn_qk_scale"].reshape(1)),
        ("wr_t", tr(a["L0_ffn_Wr"])),
        ("w1", a["L0_ffn_W1"]),
        ("b1", a["L0_ffn_b1"]),
        ("wo", a["L0_ffn_Wo"]),
        ("bo", a["L0_ffn_bo"]),
        ("gamma", a["L0_ffn_gamma"]),
        ("beta", a["L0_ffn_beta"]),
    ]
    nc = _bacc.Bacc("TRN2", target_bir_lowering=False, num_devices=1)
    arrays, args = {}, []
    for name, v in laid:
        v = _np.ascontiguousarray(v)
        arrays[f"in_{name}"] = v
        args.append(nc.dram_tensor(f"in_{name}", v.shape, _mybir.dt.from_np(v.dtype), kind="ExternalInput").ap())
    args.append(nc.dram_tensor("out_x", (B, T, C), F32, kind="ExternalOutput").ap())
    sandwich_kernel(nc, *args)
    r = _run(nc, [arrays], core_ids=[0])
    return r.results[0]["out_x"]
```

```python
import numpy as np
import concourse.bass as bass
from concourse import mybir
from contextlib import ExitStack

F32 = mybir.dt.float32
BF16 = mybir.dt.bfloat16
I32 = mybir.dt.int32
U32 = mybir.dt.uint32
ALU = mybir.AluOpType
ACT = mybir.ActivationFunctionType
AXX = mybir.AxisListType.X

P = 128
B, T, C = 8, 512, 256
H, D = 16, 16
E, FF = 8, 1024
NT = T // P
CC = C // P
FC = FF // P
TOK = B * T
TILES = TOK // P
HG = 4
G = H // HG
QKV = 3 * C
COLS = QKV + H + 1
NQK = 2 * H
SLOTS = TOK // P + E - 1
BG = 4
PER_ITER = 20
ITERS = -(-SLOTS // PER_ITER)
BLOCKS = ITERS * PER_ITER
CAPB = TOK // P + 1
ROW = 2 * C + 1
RR = 2 * BG
RW = 3
MASKED = -1e30

FA = 2.5069359320797613
FS = 0.02068334648608328
FB = -2.952890362403119
FC0 = 17.482113414249277
FSCALE = 0.42046220252761046
YMIN = float(np.log1p(0.5e-6))
SINH = [1.0 / 6, 1.0 / 120, 1.0 / 5040, 1.0 / 362880, 1.0 / 39916800, 1.0 / 6227020800]


def inverse_sqrt(nc, link, out, v, t):
    link(nc.vector.tensor_scalar(t.bitcast(I32), v.bitcast(I32), 1, None, ALU.logical_shift_right))
    link(nc.vector.tensor_scalar(out.bitcast(I32), t.bitcast(I32), -1.0, float(0x5F3759DF), ALU.mult, ALU.add))
    for _ in range(3):
        link(nc.vector.scalar_tensor_tensor(out=t, in0=v, scalar=-0.5, in1=out, op0=ALU.mult, op1=ALU.mult))
        link(nc.vector.tensor_tensor(t, t, out, ALU.mult))
        link(nc.vector.scalar_tensor_tensor(out=out, in0=t, scalar=1.5, in1=out, op0=ALU.add, op1=ALU.mult))


def units_of_group():
    out = []
    for h in (0, 2):
        for k in (h, h + 1):
            out.append([(k, 0, 0, P), (k, 2, P, 3 * P)])
            out.append([(k, 3, 0, 4 * P)])
        out.append([(h, 1, 0, 2 * P), (h + 1, 1, 2 * P, 2 * P)])
    return out


UNITS = [(g, u) for g in range(G) for u in units_of_group()]
UG = len(UNITS) // G
NU = len(UNITS)


def sandwich_kernel(nc, x, w_all, b_all, wout_t, bout, thr, log_k, qk_scale, wr_t, w1, b1, wo, bo, gamma, beta, out):
    ctx = ExitStack()
    with ctx:
        def sb(name, shape, dt=F32):
            return ctx.enter_context(nc.sbuf_tensor(name, shape, dt))

        s_sent = ctx.enter_context(nc.semaphore("rows_sent"))
        s_pad = ctx.enter_context(nc.semaphore("empty_rows_sent"))
        s_out = [ctx.enter_context(nc.semaphore(f"rows_out_{i}")) for i in range(2)]

        cleared = []

        def sem(name):
            s = ctx.enter_context(nc.semaphore(name))
            cleared.append(s.num)
            return s

        def clear_all():
            assert cleared == list(range(cleared[0], cleared[0] + len(cleared)))
            nc.all_engine_barrier(sems_to_clear=range(cleared[0], cleared[-1] + 1))

        def bc(ap, shape):
            return ap.broadcast_to(shape)

        PSH = ctx.enter_context(nc.psum_tensor("banks", [P, 8 * 512], F32))
        bank = [PSH[:, 512 * i:512 * (i + 1)] for i in range(8)]
        MB, EB, PTB = (0, 1), (2, 3), (4, 5)
        BA, BB = 6, 7

        ident = sb("ident", [P, P])
        ident_bf = sb("ident_bf", [P, P], BF16)
        mask_bf = sb("mask_bf", [P, P], BF16)
        ones = sb("ones", [P, P])
        lower = sb("lower", [P, P])
        wall = sb("wall", [P, CC, COLS])
        ball = sb("ball", [P, COLS])
        woutT = sb("woutT", [P, CC, C])
        boutB = sb("boutB", [P, C])
        wrT = sb("wrT", [P, CC, E])
        thrB = sb("thrB", [P, 1])
        logk = sb("logk", [P, H])
        lk2 = sb("lk2", [P, H])
        gcoef = sb("gcoef", [P, H])
        qks = sb("qks", [P, 1])
        safe = sb("safe", [P, 1])
        iota_i = sb("iota_i", [P, 64], I32)
        iota_e = sb("iota_e", [P, E])
        iota_k = sb("iota_k", [P, BLOCKS])
        iota_cap = sb("iota_cap", [P, E])
        iota_p = sb("iota_p", [P, 1])
        pid_i = sb("pid_i", [P, 1], I32)
        cap_i = sb("cap_i", [P, E], I32)
        fill = sb("fill", [P, ROW])

        base = sb("base", [P, E])
        idcol = sb("idcol", [P, NT], I32)

        xs_d = nc.dram_tensor("xs_scratch", ((E * CAPB + 1) * P, ROW), F32, kind="Internal").ap()

        s_w = sem("weights_loaded")
        s_fillset = sem("empty_row_set")
        s_fill = sem("empty_block_stored")
        s_act = sem("act_chain")
        s_dve = sem("dve_chain")
        s_pool = sem("pool_chain")
        s_x = sem("x_loaded")
        s_xr = sem("x_again_loaded")
        s_xn = sem("x_normalised")
        s_xT = sem("x_transposed")
        s_xnT = sem("xT_copied")
        s_proj = sem("projected")
        s_qkv = sem("qkv_biased")
        s_sq = sem("squares_ready")
        s_ez = sem("gate_exp_ready")
        s_stats = sem("ratios_ready")
        s_tok = sem("operands_built")
        s_v = sem("values_built")
        s_tokT = sem("operands_transposed")
        s_evac = sem("operands_copied")
        s_m = sem("m_ready")
        s_e = sem("e_ready")
        s_ln = sem("y_ready")
        s_a = sem("square1_ready")
        s_b = sem("square2_ready")
        s_d = sem("difference_ready")
        s_t = sem("factor_ready")
        s_f = sem("f_ready")
        s_comb = sem("scores_ready")
        s_nm = sem("max_ready")
        s_p = sem("probs_ready")
        s_pt = sem("probs_transposed")
        s_ptc = sem("probsT_copied")
        s_pv = sem("pv_done")
        s_ov = sem("pv_copied")
        s_ovT = sem("pv_transposed")
        s_ytok = sem("heads_normalised")
        s_yT = sem("heads_transposed")
        s_yTc = sem("headsT_copied")
        s_o = sem("attention_projected")
        s_on = sem("attention_normalised")
        s_or = sem("attention_read")
        s_x1 = sem("x1_ready")
        s_h = sem("h_normalised")
        s_hT = sem("h_transposed")
        s_hTc = sem("hT_copied")
        s_lg = sem("router_logits_ready")
        s_oh = sem("onehot_ready")
        s_rank = sem("ranks_ready")
        s_pos = sem("slots_ready")
        s_id = sem("numbers_ready")
        s_hb = sem("expert_h_biased")
        s_ehT = sem("expert_h_transposed")
        s_ehTc = sem("expert_hT_copied")
        s_up = sem("expert_up_ready")
        s_gelu = sem("gelu_ready")
        s_down = sem("expert_down_ready")
        s_sum = sem("down_read")
        s_n1 = sem("first_norm_ready")
        s_gb = sem("gamma_beta_ready")
        s_n2 = sem("second_norm_ready")
        s_res = sem("expert_rows_ready")
        s_rows = [sem(f"rows_loaded_{i}") for i in range(RR)]
        s_w1 = [sem(f"expert_loaded_{i}") for i in range(RW)]

        NW = 16 * (3 * CC + 5)
        with nc.Block() as block:
            @block.sync
            def _(sp):
                for c in range(CC):
                    sp.dma_start(wall[:, c, :], w_all[c * P:(c + 1) * P, :]).then_inc(s_w, 16)
                    sp.dma_start(woutT[:, c, :], wout_t[c * P:(c + 1) * P, :]).then_inc(s_w, 16)
                    sp.dma_start(wrT[:, c, :], wr_t[c * P:(c + 1) * P, :]).then_inc(s_w, 16)
                sp.dma_start(ball[:, :], b_all.partition_broadcast(P)).then_inc(s_w, 16)
                sp.dma_start(boutB[:, :], bout.partition_broadcast(P)).then_inc(s_w, 16)
                sp.dma_start(thrB[:, :], thr.partition_broadcast(P)).then_inc(s_w, 16)
                sp.dma_start(logk[:, :], log_k.partition_broadcast(P)).then_inc(s_w, 16)
                sp.dma_start(qks[:, :], qk_scale.partition_broadcast(P)).then_inc(s_w, 16)
                sp.wait_ge(s_fillset, 1)
                sp.dma_start(xs_d[E * CAPB * P:(E * CAPB + 1) * P, :], fill[:, :]).then_inc(s_fill, 16)
                sp.wait_ge(s_w, NW)
                sp.wait_ge(s_fill, 16)

            @block.gpsimd
            def _(pool):
                n = [0]

                def link(ins):
                    n[0] += 1
                    ins.then_inc(s_pool, 1)
                    pool.wait_ge(s_pool, n[0])

                nc.gpsimd.memset(fill[:, 0:2 * C], 0.0)
                nc.gpsimd.memset(fill[:, 2 * C:ROW].bitcast(I32), TOK).then_inc(s_fillset, 1)
                nc.gpsimd.memset(ones[:, :], 1.0)
                nc.gpsimd.memset(ident[:, :], 0.0)
                nc.gpsimd.memset(ident_bf[:, :], 0.0)
                link(nc.gpsimd.memset(mask_bf[:, :], 0.0))
                nc.gpsimd.affine_select(out=ident[:, :], in_=ident[:, :], compare_op=ALU.not_equal, fill=1.0,
                                        base=0, pattern=[[-1, P]], channel_multiplier=1)
                nc.gpsimd.affine_select(out=ident_bf[:, :], in_=ident_bf[:, :], compare_op=ALU.not_equal, fill=1.0,
                                        base=0, pattern=[[-1, P]], channel_multiplier=1)
                nc.gpsimd.affine_select(out=mask_bf[:, :], in_=mask_bf[:, :], compare_op=ALU.is_ge, fill=MASKED,
                                        base=0, pattern=[[-1, P]], channel_multiplier=1)
                nc.gpsimd.affine_select(out=lower[:, :], in_=ones[:, :], compare_op=ALU.is_gt, fill=0.0,
                                        base=0, pattern=[[1, P]], channel_multiplier=-1)
                nc.gpsimd.iota(idcol[:, :], pattern=[[P, NT]], base=0, channel_multiplier=1)
                nc.gpsimd.iota(pid_i[:, :], pattern=[[1, 1]], base=0, channel_multiplier=1)
                nc.gpsimd.iota(cap_i[:, :], pattern=[[CAPB * P, E]], base=0, channel_multiplier=0)
                link(nc.gpsimd.iota(iota_i[:, 0:BLOCKS], pattern=[[1, BLOCKS]], base=0, channel_multiplier=0))
                nc.gpsimd.tensor_copy(iota_k[:, :], iota_i[:, 0:BLOCKS])
                nc.gpsimd.tensor_copy(iota_e[:, :], iota_i[:, 0:E])
                nc.gpsimd.tensor_copy(iota_p[:, :], pid_i[:, :])
                nc.gpsimd.tensor_copy(base[:, :], cap_i[:, :])
                link(nc.gpsimd.tensor_copy(iota_cap[:, :], cap_i[:, :]))

            @block.scalar
            def _(act):
                nc.scalar.preload_act_table_set("natural_log_exp_and_others")
                act.wait_ge(s_w, NW)
                nc.scalar.activation(safe[:, :], qks[:, :], ACT.Exp, scale=-1.0).then_inc(s_act, 1)
                act.wait_ge(s_dve, 1)
                nc.scalar.activation(lk2[:, :], gcoef[:, :], ACT.Exp, scale=-1.0).then_inc(s_act, 1)
                act.wait_ge(s_act, 2)
                nc.scalar.activation(gcoef[:, :], lk2[:, :], ACT.Ln, bias=1.0).then_inc(s_act, 1)

            @block.vector
            def _(dve):
                n = [0]

                def link(ins):
                    n[0] += 1
                    ins.then_inc(s_dve, 1)
                    dve.wait_ge(s_dve, n[0])

                dve.wait_ge(s_w, NW)
                link(nc.vector.scalar_tensor_tensor(out=gcoef[:, :], in0=logk[:, :], scalar=-1.0, in1=logk[:, :],
                                                    op0=ALU.mult, op1=ALU.max))
                dve.wait_ge(s_act, 1)
                link(nc.vector.tensor_scalar(safe[:, :], safe[:, :], 1.0, None, ALU.add))
                link(nc.vector.reciprocal(safe[:, :], safe[:, :]))
                link(nc.vector.tensor_scalar(safe[:, :], safe[:, :], 1.5, None, ALU.mult))
                dve.wait_ge(s_act, 3)
                link(nc.vector.scalar_tensor_tensor(out=lk2[:, :], in0=logk[:, :], scalar=0.0, in1=gcoef[:, :],
                                                    op0=ALU.max, op1=ALU.add))
                link(nc.vector.tensor_scalar(lk2[:, :], lk2[:, :], 1e-6, None, ALU.add))
                link(nc.vector.reciprocal(lk2[:, :], lk2[:, :]))
                link(nc.vector.tensor_scalar(gcoef[:, :], lk2[:, :], -FSCALE, None, ALU.mult))
        clear_all()

        actx = ExitStack()

        def ab(name, shape, dt=F32):
            return actx.enter_context(nc.sbuf_tensor(name, shape, dt))

        x_sb = ab("x_sb", [P, NT, C])
        xnT = ab("xnT", [P, CC, T])
        st6 = ab("st6", [P, NT, 6])
        mv = ab("mv", [P, NT, 2])
        rstd = ab("rstd", [P, NT])
        vare = ab("vare", [P, NT])
        rtmp = ab("rtmp", [P, NT])
        qkv = ab("qkv", [P, NT, COLS])
        sqb = ab("sqb", [P, NT, NQK, D])
        ez = ab("ez", [P, NT, H + 1])
        spike = ab("spike", [P, NT])
        spike_next = ab("spike_next", [P, NT])
        ga = ab("ga", [P, NT, H])
        ga_next = ab("ga_next", [P, NT, H])
        be = ab("be", [P, NT, H])
        small = [ab(f"small{i}", [P, NT, NQK]) for i in range(7)]
        ratio = ab("ratio", [P, NT, NQK])
        time_ = ab("time_", [P, NT, NQK])
        tokQ = ab("tokQ", [P, NT, HG, 2 * D])
        tokE = ab("tokE", [P, NT, HG, 2 * D])
        tokM = ab("tokM", [P, NT, HG, 2 * D])
        vaug = [ab(f"vaug{i}", [P, NT, HG, 2 * D]) for i in range(G)]
        Qz = [ab(f"Qz{i}", [P, HG, T]) for i in range(2)]
        KE = [ab(f"KE{i}", [P, T]) for i in range(2)]
        KM = [ab(f"KM{i}", [P, T]) for i in range(2)]
        RY = 4
        yR = [ab(f"yR{i}", [P, 512]) for i in range(RY)]
        aR = [ab(f"aR{i}", [P, 512]) for i in range(2)]
        wR = [ab(f"wR{i}", [P, 512]) for i in range(2)]
        dR = [ab(f"dR{i}", [P, 512]) for i in range(2)]
        tR = [ab(f"tR{i}", [P, 512]) for i in range(2)]
        fR = [ab(f"fR{i}", [P, 512]) for i in range(2)]
        sR = [ab(f"sR{i}", [P, 512]) for i in range(3)]
        pR = [ab(f"pR{i}", [P, 512]) for i in range(3)]
        nm = ab("nm", [P, 4, 2])
        PT = ab("PT", [P, HG, NT, NT, P])
        ov = ab("ov", [P, T])
        rs = ab("rs", [P, NT, HG])
        ytok = ab("ytok", [P, NT, C])
        xr = ab("xr", [P, NT, C])
        ob = ab("ob", [P, NT, C])
        xrow = ab("xrow", [P, NT, ROW])
        lgs = ab("lgs", [P, NT, E])
        mx8 = ab("mx8", [P, NT, 8])
        ix8 = ab("ix8", [P, NT, 8], U32)
        exf = ab("exf", [P, NT])
        onehot = ab("onehot", [P, NT, E])
        run = ab("run", [P, NT, E])
        posf = ab("posf", [P, NT])
        pos = ab("pos", [P, NT], I32)

        with nc.Block() as block:
            @block.vector
            def _(dve):
                for t in (tokE, tokM):
                    nc.vector.memset(t[:, :, :, :], 0.0)
                for i in range(2):
                    nc.vector.memset(Qz[i][:, :, :], 0.0)
                for i in range(G):
                    last = nc.vector.memset(vaug[i][:, :, :, :], 0.0)
                last.then_inc(s_dve, 1)
                dve.wait_ge(s_dve, 1)
                for i in range(G):
                    nc.vector.memset(vaug[i][:, :, :, D:D + 1], 1.0)
        clear_all()

        x_v = x.rearrange("b (t p) c -> b p t c", p=P)

        def batch_of(b):
            one = x_v[b:b + 1] if isinstance(b, int) else x_v[bass.ds(b, 1)]
            return one.rearrange("o p t c -> p (o t) c")

        BUILD_AT = {0: 1, UG - 1: 2, 2 * UG - 1: 3, 3 * UG + 2: G}
        LAST = NU + 7

        def turn(b, units, head, tail):
            preps = (list(range(1, G)) if units else []) + ([G] if head else [])

            with nc.Block() as block:
                @block.sync
                def _(sp):
                    if tail:
                        sp.dma_start(xr[:, :, :], batch_of(b - 1)).then_inc(s_xr, 16)
                    if head:
                        sp.dma_start(x_sb[:, :, :], batch_of(b + 1)).then_inc(s_x, 16)

                @block.vector
                def _(dve):
                    n = [0]

                    def link(ins):
                        n[0] += 1
                        ins.then_inc(s_dve, 1)
                        dve.wait_ge(s_dve, n[0])

                    def row_stats(rows_of):
                        for j in range(NT):
                            last = nc.vector.bn_stats(st6[:, j, :], rows_of(j))
                        link(last)
                        for j in range(NT):
                            last = nc.vector.bn_aggr(mv[:, j, :], st6[:, j, :])
                        link(last)

                    def row_scale(eps):
                        link(nc.vector.tensor_scalar(vare[:, :], mv[:, :, 1], eps, None, ALU.add))
                        inverse_sqrt(nc, link, rstd[:, :], vare[:, :], rtmp[:, :])

                    def normalise(dst_of, rows_of, signal):
                        for j in range(NT):
                            last = nc.vector.tensor_scalar(dst_of(j), rows_of(j), mv[:, j, 0:1], rstd[:, j:j + 1],
                                                           ALU.subtract, ALU.mult)
                        last.then_inc(signal, 1)

                    def distance(k):
                        dve.wait_ge(s_t, k + 1)
                        if k >= 2:
                            dve.wait_ge(s_comb, k - 1)
                        nc.vector.scalar_tensor_tensor(out=fR[k % 2][:, :], in0=yR[k % RY][:, :], scalar=YMIN,
                                                       in1=tR[k % 2][:, :], op0=ALU.max, op1=ALU.mult).then_inc(s_f, 1)

                    def scores(k):
                        g, unit = UNITS[k]
                        dve.wait_ge(s_f, k + 1)
                        dve.wait_ge(s_e, k + 1)
                        if k >= 3:
                            dve.wait_ge(s_p, k - 2)
                        for h, t, off, w in unit:
                            last = nc.vector.scalar_tensor_tensor(
                                out=sR[k % 3][:, off:off + w], in0=fR[k % 2][:, off:off + w],
                                scalar=ga[:, t, g * HG + h:g * HG + h + 1], in1=bank[EB[k % 2]][:, off:off + w],
                                op0=ALU.mult, op1=ALU.add)
                        last.then_inc(s_comb, 1)

                    def maxima(k):
                        dve.wait_ge(s_comb, k + 1)
                        for i, (h, t, off, w) in enumerate(UNITS[k][1]):
                            last = nc.vector.tensor_reduce(nm[:, k % 4, i:i + 1], sR[k % 3][:, off:off + w], AXX,
                                                           ALU.max, negate=True)
                        last.then_inc(s_nm, 1)

                    def keep_probsT(k):
                        g, unit = UNITS[k]
                        dve.wait_ge(s_pt, k + 1)
                        if k % UG == 0 and g >= 1:
                            dve.wait_ge(s_pv, g)
                        src = bank[PTB[k % 2]]
                        if len(unit) == 2 and unit[0][1] == 1:
                            h = unit[0][0]
                            last = nc.vector.tensor_copy(PT[:, h:h + 2, 0:2, 1, :],
                                                         src.rearrange("p (h j q) -> p h j q", h=2, j=2))
                        else:
                            for h, t, off, w in unit:
                                last = nc.vector.tensor_copy(PT[:, h, 0:t + 1, t, :],
                                                             src[:, off:off + w].rearrange("p (j q) -> p j q", q=P))
                        last.then_inc(s_ptc, 1)

                    def heads(g):
                        dve.wait_ge(s_ovT, g + 1)
                        v = bank[BA].rearrange("p (t h d) -> p t h d", t=NT, h=HG)
                        link(nc.vector.reciprocal(rs[:, :, :], v[:, :, :, D]))
                        link(nc.vector.tensor_tensor(rs[:, :, :], rs[:, :, :],
                                                     bc(spike[:, :].unsqueeze(2), [P, NT, HG]), ALU.mult))
                        dst = ytok[:, :, g * HG * D:(g + 1) * HG * D].rearrange("p t (h d) -> p t h d", h=HG)
                        nc.vector.tensor_tensor(dst, v[:, :, :, 0:D], bc(rs[:, :, :].unsqueeze(3), [P, NT, HG, D]),
                                                ALU.mult).then_inc(s_ytok, 1)

                    ob_of = lambda j: ob[:, j, :]
                    x1_of = lambda j: xrow[:, j, 0:C]
                    h_of = lambda j: xrow[:, j, C:2 * C]

                    def tail_bias():
                        dve.wait_ge(s_o, NT)
                        nc.vector.tensor_tensor(ob[:, :, :], PSH[:, 512 * BA:512 * (BA + 2)].rearrange(
                            "p (t c) -> p t c", t=NT), bc(boutB[:, :].unsqueeze(1), [P, NT, C]),
                            ALU.add).then_inc(s_or, 1)
                        dve.wait_ge(s_or, 1)
                        row_stats(ob_of)

                    def tail_norm():
                        row_scale(1e-5)
                        normalise(ob_of, ob_of, s_on)

                    def tail_norm2():
                        dve.wait_ge(s_x1, 1)
                        row_stats(x1_of)
                        row_scale(1e-5)

                    def tail_h():
                        normalise(h_of, x1_of, s_h)

                    def tail_route():
                        dve.wait_ge(s_lg, 1)
                        link(nc.vector.tensor_copy(lgs[:, :, :],
                                                   bank[BA][:, 0:NT * E].rearrange("p (t e) -> p t e", t=NT)))
                        for j in range(NT):
                            last = nc.vector.max(mx8[:, j, :], lgs[:, j, :])
                        link(last)
                        for j in range(NT):
                            last = nc.vector.max_index(ix8[:, j, :], mx8[:, j, :], lgs[:, j, :])
                        link(last)
                        link(nc.vector.tensor_copy(exf[:, :], ix8[:, :, 0]))
                        nc.vector.tensor_tensor(onehot[:, :, :], bc(exf[:, :].unsqueeze(2), [P, NT, E]),
                                                bc(iota_e[:, :].unsqueeze(1), [P, NT, E]), ALU.is_equal
                                                ).then_inc(s_oh, 1)

                    def tail_slots():
                        dve.wait_ge(s_rank, 1)
                        rank = bank[BA][:, 64:64 + NT * E].rearrange("p (t e) -> p t e", t=NT)
                        tot = bank[BA][:, 128:128 + NT * E].rearrange("p (t e) -> p t e", t=NT)
                        link(nc.vector.tensor_copy(run[:, 0, :], base[:, :]))
                        for j in range(1, NT):
                            link(nc.vector.tensor_tensor(run[:, j, :], run[:, j - 1, :], tot[:, j - 1, :], ALU.add))
                        link(nc.vector.tensor_tensor(base[:, :], run[:, NT - 1, :], tot[:, NT - 1, :], ALU.add))
                        link(nc.vector.tensor_tensor(run[:, :, :], run[:, :, :], rank, ALU.add))
                        link(nc.vector.tensor_tensor(run[:, :, :], run[:, :, :], onehot[:, :, :], ALU.mult))
                        link(nc.vector.reduce_sum(posf[:, :], run[:, :, :], AXX))
                        nc.vector.tensor_copy(pos[:, :], posf[:, :]).then_inc(s_pos, 1)
                        dve.wait_ge(s_id, 1)
                        nc.vector.tensor_scalar(idcol[:, :], idcol[:, :], float(T), None, ALU.add)

                    x_of = lambda j: x_sb[:, j, :]

                    def head_stats():
                        dve.wait_ge(s_x, 16)
                        row_stats(x_of)

                    def head_norm():
                        row_scale(1e-5)
                        normalise(x_of, x_of, s_xn)

                    def head_bias(j):
                        dve.wait_ge(s_proj, j + 1)
                        if units and j == 0:
                            dve.wait_ge(s_tok, 6 * (G - 1))
                            dve.wait_ge(s_v, G - 1)
                        nc.vector.tensor_tensor(qkv[:, j, :], PSH[:, 512 * BA:512 * BA + COLS], ball[:, :],
                                                ALU.add).then_inc(s_qkv, 1)

                    def head_gates():
                        dve.wait_ge(s_ez, 1)
                        link(nc.vector.tensor_scalar(ez[:, :, :], ez[:, :, :], 1.0, None, ALU.add))
                        link(nc.vector.reciprocal(ez[:, :, :], ez[:, :, :]))
                        nc.vector.tensor_scalar(spike_next[:, :], ez[:, :, H], thrB[:, 0:1], None, ALU.is_gt)
                        nc.vector.tensor_tensor(ga_next[:, :, :], ez[:, :, 0:H],
                                                bc(gcoef[:, :].unsqueeze(1), [P, NT, H]), ALU.mult)
                        nc.vector.tensor_scalar(be[:, :, :], ez[:, :, 0:H], -0.25, 0.25, ALU.mult, ALU.add)

                    ss, inv, i2, z, r, sp2, t2 = [s[:, :, :] for s in small]
                    q0 = sqb[:, :, :, 0]

                    def head_sums():
                        dve.wait_ge(s_sq, 1)
                        link(nc.vector.reduce_sum(ss, sqb[:, :, :, :], AXX))
                        nc.vector.tensor_scalar(t2, ss, 1e-24, None, ALU.max)
                        nc.vector.tensor_tensor(sp2, ss, q0, ALU.subtract)
                        link(nc.vector.scalar_tensor_tensor(out=z, in0=q0, scalar=-2.0, in1=ss, op0=ALU.mult,
                                                            op1=ALU.add))

                    def head_inverse_norms():
                        inverse_sqrt(nc, link, inv, t2, i2)

                    def head_ratios():
                        link(nc.vector.tensor_scalar(inv, inv, safe[:, 0:1], None, ALU.mult))
                        link(nc.vector.tensor_tensor(i2, inv, inv, ALU.mult))
                        link(nc.vector.tensor_tensor(z, z, i2, ALU.mult))
                        link(nc.vector.tensor_scalar(z, z, 1e-8, None, ALU.max))
                        link(nc.vector.tensor_scalar(r, z, SINH[-1], None, ALU.mult))
                        for c in SINH[-2::-1]:
                            link(nc.vector.scalar_tensor_tensor(out=r, in0=r, scalar=c, in1=z, op0=ALU.add,
                                                                op1=ALU.mult))
                        link(nc.vector.scalar_tensor_tensor(out=r, in0=r, scalar=1.0, in1=inv, op0=ALU.add,
                                                            op1=ALU.mult))

                    def head_times():
                        link(nc.vector.tensor_tensor(t2, r, r, ALU.mult))
                        nc.vector.tensor_copy(ratio[:, :, 0:H], r[:, :, 0:H])
                        nc.vector.tensor_scalar(ratio[:, :, H:NQK], r[:, :, H:NQK], -1.0, None, ALU.mult)
                        link(nc.vector.tensor_tensor(t2, t2, sp2, ALU.mult))
                        link(nc.vector.tensor_scalar(t2, t2, 1.0, None, ALU.add))

                    def head_times2():
                        inverse_sqrt(nc, link, i2, t2, z)
                        nc.vector.tensor_tensor(time_[:, :, :], t2, i2, ALU.mult).then_inc(s_stats, 1)

                    if units:
                        nc.vector.tensor_copy(spike[:, :], spike_next[:, :])
                        link(nc.vector.tensor_copy(ga[:, :, :], ga_next[:, :, :]))
                    for k in range(LAST):
                        if units and 2 <= k < NU + 2:
                            distance(k - 2)
                        if units and 5 <= k < NU + 5:
                            keep_probsT(k - 5)
                        if units and 2 <= k < NU + 2:
                            scores(k - 2)
                            maxima(k - 2)
                        if units and k >= UG + 6 and (k - 6) % UG == 0:
                            heads((k - 6) // UG - 1)
                        if tail and k == 3:
                            tail_bias()
                        if tail and k == 4:
                            tail_norm()
                        if tail and k == 6:
                            tail_norm2()
                        if tail and k == 7:
                            tail_h()
                        if tail and k == 12:
                            tail_route()
                        if tail and k == 14:
                            tail_slots()
                        if head and k == 17:
                            head_stats()
                        if head and k == 18:
                            head_norm()
                        if head and 21 <= k < 21 + NT:
                            head_bias(k - 21)
                        if head and k == 26:
                            head_gates()
                        if head and k == 27:
                            head_sums()
                        if head and k == 28:
                            head_inverse_norms()
                        if head and k == 29:
                            head_ratios()
                        if head and k == 30:
                            head_times()
                        if head and k == 31:
                            head_times2()

                @block.scalar
                def _(act):
                    def copy_operands_qe(g):
                        i, at = g % 2, preps.index(g)
                        if units and g >= 2:
                            act.wait_ge(s_e, UG * (g - 1))
                        act.wait_ge(s_tokT, 3 * at + 1)
                        for h in range(HG):
                            rows = slice(2 * D * h, 2 * D * (h + 1))
                            last = nc.scalar.copy(Qz[i][rows, h, :], bank[BA][rows, :])
                        last.then_inc(s_evac, 1)
                        act.wait_ge(s_tokT, 3 * at + 2)
                        nc.scalar.copy(KE[i][:, :], bank[BB]).then_inc(s_evac, 1)

                    def copy_operands_m(g):
                        act.wait_ge(s_tokT, 3 * preps.index(g) + 3)
                        nc.scalar.copy(KM[g % 2][:, :], bank[BA]).then_inc(s_evac, 1)

                    def log(k):
                        act.wait_ge(s_m, k + 1)
                        if k >= RY:
                            act.wait_ge(s_f, k - RY + 1)
                        nc.scalar.activation(yR[k % RY][:, :], bank[MB[k % 2]], ACT.Ln, bias=0.5,
                                             scale=0.5).then_inc(s_ln, 1)

                    def square1(k):
                        act.wait_ge(s_ln, k + 1)
                        if k >= 2:
                            act.wait_ge(s_b, k - 1)
                        nc.scalar.activation(aR[k % 2][:, :], yR[k % RY][:, :], ACT.Square, bias=FA).then_inc(s_a, 1)

                    def square2(k):
                        act.wait_ge(s_a, k + 1)
                        if k >= 2:
                            act.wait_ge(s_d, k - 1)
                        nc.scalar.activation(wR[k % 2][:, :], aR[k % 2][:, :], ACT.Square, bias=FB,
                                             scale=FS).then_inc(s_b, 1)

                    def probs(k):
                        act.wait_ge(s_nm, k + 1)
                        if k >= 3:
                            act.wait_ge(s_pt, k - 2)
                        for i, (h, t, off, w) in enumerate(UNITS[k][1]):
                            last = nc.scalar.activation(pR[k % 3][:, off:off + w], sR[k % 3][:, off:off + w], ACT.Exp,
                                                        bias=nm[:, k % 4, i:i + 1])
                        last.then_inc(s_p, 1)

                    def copy_pv(g):
                        act.wait_ge(s_pv, g + 1)
                        if g >= 1:
                            act.wait_ge(s_ovT, g)
                        nc.scalar.copy(ov[:, :], bank[BB]).then_inc(s_ov, 1)

                    def copy_transposed(ready, done):
                        for c in range(CC):
                            act.wait_ge(ready, c + 1)
                            nc.scalar.copy(xnT[:, c, :], bank[BA + c]).then_inc(done, 1)

                    for k in range(LAST):
                        if units and k < NU:
                            log(k)
                        if units and 3 <= k < NU + 3:
                            probs(k - 3)
                        if units and k < NU:
                            square1(k)
                        if tail and k == 0:
                            copy_transposed(s_yT, s_yTc)
                        if tail and k == 10:
                            copy_transposed(s_hT, s_hTc)
                        if head and k == 20:
                            copy_transposed(s_xT, s_xnT)
                        if k % UG == 8 and k // UG + 1 in preps:
                            copy_operands_qe(k // UG + 1)
                        if k % UG == 9 and k // UG + 1 in preps:
                            copy_operands_m(k // UG + 1)
                        if head and k == 25:
                            act.wait_ge(s_qkv, NT)
                            nc.scalar.activation(ez[:, :, :], qkv[:, :, QKV:COLS], ACT.Exp,
                                                 scale=-1.0).then_inc(s_ez, 1)
                        if head and k == 26:
                            nc.scalar.activation(sqb[:, :, :, :].rearrange("p t n d -> p t (n d)"),
                                                 qkv[:, :, 0:2 * C], ACT.Square).then_inc(s_sq, 1)
                        if units and k >= UG + 5 and (k - 5) % UG == 0:
                            copy_pv((k - 5) // UG - 1)
                        if units and k < NU:
                            square2(k)

                @block.gpsimd
                def _(pool):
                    def part(col, g):
                        at = col + g % G * HG * D
                        return qkv[:, :, at:at + HG * D].rearrange("p t (h d) -> p t h d", h=HG)

                    def build(g):
                        hq = slice(g % G * HG, (g % G + 1) * HG)
                        hk = slice(H + g % G * HG, H + (g % G + 1) * HG)
                        q, kk = part(0, g), part(C, g)
                        if g == G:
                            pool.wait_ge(s_stats, 1)
                        if preps.index(g) >= 1:
                            pool.wait_ge(s_tokT, 3 * preps.index(g))
                        S = [P, NT, HG, D]
                        S1 = [P, NT, HG, D - 1]
                        nc.gpsimd.tensor_tensor(tokQ[:, :, :, 0:D], q, bc(be[:, :, hq].unsqueeze(3), S),
                                                ALU.mult).then_inc(s_tok, 1)
                        nc.gpsimd.tensor_tensor(tokQ[:, :, :, D + 1:2 * D], q[:, :, :, 1:D],
                                                bc(ratio[:, :, hq].unsqueeze(3), S1), ALU.mult).then_inc(s_tok, 1)
                        nc.gpsimd.tensor_copy(tokQ[:, :, :, D], time_[:, :, hq]).then_inc(s_tok, 1)
                        nc.gpsimd.tensor_copy(tokE[:, :, :, 0:D], kk).then_inc(s_tok, 1)
                        nc.gpsimd.tensor_tensor(tokM[:, :, :, D + 1:2 * D], kk[:, :, :, 1:D],
                                                bc(ratio[:, :, hk].unsqueeze(3), S1), ALU.mult).then_inc(s_tok, 1)
                        nc.gpsimd.tensor_copy(tokM[:, :, :, D], time_[:, :, hk]).then_inc(s_tok, 1)
                        if units and g == G:
                            pool.wait_ge(s_pv, 1)
                        nc.gpsimd.tensor_copy(vaug[g % G][:, :, :, 0:D], part(2 * C, g)).then_inc(s_v, 1)

                    def difference(k):
                        pool.wait_ge(s_b, k + 1)
                        if k >= 2:
                            pool.wait_ge(s_t, k - 1)
                        nc.gpsimd.tensor_tensor(dR[k % 2][:, :], yR[k % RY][:, :], wR[k % 2][:, :],
                                                ALU.subtract).then_inc(s_d, 1)

                    def factor(k):
                        pool.wait_ge(s_d, k + 1)
                        if k >= 2:
                            pool.wait_ge(s_f, k - 1)
                        nc.gpsimd.tensor_scalar(tR[k % 2][:, :], dR[k % 2][:, :], 1.0, FC0, ALU.mult,
                                                ALU.add).then_inc(s_t, 1)

                    for k in range(LAST):
                        if units and k < NU:
                            difference(k)
                            factor(k)
                        if tail and k == 0:
                            nc.gpsimd.tensor_copy(xrow[:, :, 2 * C].bitcast(I32), idcol[:, :]).then_inc(s_id, 1)
                        if tail and k == 4:
                            pool.wait_ge(s_on, 1)
                            pool.wait_ge(s_xr, 16)
                            nc.gpsimd.tensor_tensor(xrow[:, :, 0:C], xr[:, :, :], ob[:, :, :],
                                                    ALU.add).then_inc(s_x1, 1)
                        if tail and k == 15:
                            pool.wait_ge(s_pos, 1)
                            pool.wait_ge(s_h, 1)
                            pool.wait_ge(s_id, 1)
                            for j in range(NT):
                                pool.indirect_dma_start(
                                    out=xs_d, out_offset=bass.IndirectOffsetOnAxis(ap=pos[:, j:j + 1], axis=0),
                                    in_=xrow[:, j, :], in_offset=None).then_inc(s_sent, 16)
                        g = BUILD_AT.get(k)
                        if g in preps:
                            build(g)
                    if tail:
                        pool.wait_ge(s_sent, b * (16 * NT))

                @block.tensor
                def _(pe):
                    def transpose_into(dst, src):
                        for j in range(NT):
                            last = nc.tensor.transpose(bank[dst][:, j * P:(j + 1) * P],
                                                       src[:, j, :, :].rearrange("p h d -> p (h d)"), ident[:, :])
                        last.then_inc(s_tokT, 1)

                    def transpose_operands_qe(g):
                        at = preps.index(g)
                        pe.wait_ge(s_tok, 6 * (at + 1))
                        if at >= 1:
                            pe.wait_ge(s_evac, 3 * at)
                        if g >= 2 and units:
                            pe.wait_ge(s_ytok, g - 1)
                            pe.wait_ge(s_ov, g - 1)
                        if g == 1 and tail:
                            pe.wait_ge(s_or, 1)
                        if g == G:
                            pe.wait_ge(s_qkv, NT)
                        transpose_into(BA, tokQ)
                        transpose_into(BB, tokE)

                    def transpose_operands_m(g):
                        pe.wait_ge(s_evac, 3 * preps.index(g) + 1)
                        transpose_into(BA, tokM)

                    def lorentz(k):
                        g, unit = UNITS[k]
                        if k % UG == 0 and g >= 1:
                            pe.wait_ge(s_evac, 3 * g)
                        if k >= 2:
                            pe.wait_ge(s_ln, k - 1)
                        for h, t, off, w in unit:
                            last = nc.tensor.matmul(bank[MB[k % 2]][:, off:off + w],
                                                    Qz[g % 2][:, h, t * P:(t + 1) * P], KM[g % 2][:, 0:w],
                                                    start=True, stop=True)
                        last.then_inc(s_m, 1)

                    def dots(k):
                        g, unit = UNITS[k]
                        if k >= 2:
                            pe.wait_ge(s_comb, k - 1)
                        for h, t, off, w in unit:
                            dst = bank[EB[k % 2]]
                            nc.tensor.matmul(dst[:, off:off + w], Qz[g % 2][:, h, t * P:(t + 1) * P],
                                             KE[g % 2][:, 0:w], start=True, stop=False)
                            last = nc.tensor.matmul(dst[:, off + w - P:off + w], ident_bf[:, :], mask_bf[:, :],
                                                    start=False, stop=True)
                        last.then_inc(s_e, 1)

                    def transpose_probs(k):
                        pe.wait_ge(s_p, k + 1)
                        if k >= 2:
                            pe.wait_ge(s_ptc, k - 1)
                        for j in range(4):
                            last = nc.tensor.transpose(bank[PTB[k % 2]][:, j * P:(j + 1) * P],
                                                       pR[k % 3][:, j * P:(j + 1) * P], ident[:, :])
                        last.then_inc(s_pt, 1)

                    def values(g):
                        if g >= 1:
                            pe.wait_ge(s_v, g)
                        pe.wait_ge(s_ptc, UG * (g + 1))
                        if preps[:g + 1]:
                            pe.wait_ge(s_evac, 3 * len(preps[:g + 1]))
                        if g >= 1:
                            pe.wait_ge(s_ov, g)
                        if g == 1 and head:
                            pe.wait_ge(s_qkv, NT)
                        for j in range(NT):
                            for h in range(HG):
                                last = nc.tensor.matmul(bank[BB][2 * D * h:2 * D * (h + 1), j * P:T],
                                                        vaug[g][:, j, h, :],
                                                        PT[:, h, j, j:NT, :].rearrange("p t q -> p (t q)"),
                                                        start=(j == 0), stop=(j == NT - 1),
                                                        tile_position=(0, 2 * D * h), skip_group_check=True)
                        last.then_inc(s_pv, 1)

                    def transpose_values(g):
                        pe.wait_ge(s_ov, g + 1)
                        if g >= 1:
                            pe.wait_ge(s_ytok, g)
                        if g == 0 and tail:
                            pe.wait_ge(s_pos, 1)
                        for j in range(NT):
                            last = nc.tensor.transpose(bank[BA][:, j * P:(j + 1) * P], ov[:, j * P:(j + 1) * P],
                                                       ident[:, :])
                        last.then_inc(s_ovT, 1)

                    def transpose_rows(rows_of, signal):
                        for c in range(CC):
                            for j in range(NT):
                                last = nc.tensor.transpose(bank[BA + c][:, j * P:(j + 1) * P],
                                                           rows_of(j)[:, c * P:(c + 1) * P], ident[:, :])
                            last.then_inc(signal, 1)

                    def project_out():
                        pe.wait_ge(s_yTc, CC)
                        for j in range(NT):
                            for c in range(CC):
                                last = nc.tensor.matmul(bank[BA + j // 2][:, (j % 2) * C:(j % 2 + 1) * C],
                                                        xnT[:, c, j * P:(j + 1) * P], woutT[:, c, :],
                                                        start=(c == 0), stop=(c == CC - 1))
                            last.then_inc(s_o, 1)

                    def route():
                        pe.wait_ge(s_hTc, CC)
                        for j in range(NT):
                            for c in range(CC):
                                last = nc.tensor.matmul(bank[BA][:, j * E:(j + 1) * E], xnT[:, c, j * P:(j + 1) * P],
                                                        wrT[:, c, :], start=(c == 0), stop=(c == CC - 1))
                        last.then_inc(s_lg, 1)

                    def rank():
                        pe.wait_ge(s_oh, 1)
                        oh = onehot[:, :, :].rearrange("p i e -> p (i e)")
                        nc.tensor.matmul(bank[BA][:, 64:64 + NT * E], lower[:, :], oh, start=True, stop=True)
                        nc.tensor.matmul(bank[BA][:, 128:128 + NT * E], ones[:, :], oh, start=True,
                                         stop=True).then_inc(s_rank, 1)

                    def project(j):
                        pe.wait_ge(s_xnT, CC)
                        if j >= 1:
                            pe.wait_ge(s_qkv, j)
                        for dst, c0, c1 in ((BA, 0, 512), (BB, 512, COLS)):
                            for c in range(CC):
                                last = nc.tensor.matmul(bank[dst][:, 0:c1 - c0], xnT[:, c, j * P:(j + 1) * P],
                                                        wall[:, c, c0:c1], start=(c == 0), stop=(c == CC - 1))
                        last.then_inc(s_proj, 1)

                    for k in range(LAST):
                        if units and k < NU:
                            lorentz(k)
                        if units and 1 <= k <= NU:
                            dots(k - 1)
                        if units and 4 <= k < NU + 4:
                            transpose_probs(k - 4)
                        if tail and k == 0:
                            transpose_rows(lambda j: ytok[:, j, :], s_yT)
                        if tail and k == 2:
                            project_out()
                        if tail and k == 10:
                            pe.wait_ge(s_h, 1)
                            if units:
                                pe.wait_ge(s_evac, 3)
                            transpose_rows(lambda j: xrow[:, j, C:2 * C], s_hT)
                        if tail and k == 12:
                            route()
                        if tail and k == 13:
                            rank()
                        if head and k == 20:
                            pe.wait_ge(s_xn, 1)
                            if units:
                                pe.wait_ge(s_evac, 6)
                                pe.wait_ge(s_ov, 1)
                            transpose_rows(lambda j: x_sb[:, j, :], s_xT)
                        if head and 21 <= k < 21 + NT:
                            project(k - 21)
                        if k % UG == 7 and k // UG + 1 in preps:
                            transpose_operands_qe(k // UG + 1)
                        if k % UG == 8 and k // UG + 1 in preps:
                            transpose_operands_m(k // UG + 1)
                        if units and k >= UG + 5 and (k - 5) % UG == 0:
                            values((k - 5) // UG - 1)
                        if units and k >= UG + 6 and (k - 6) % UG == 0:
                            transpose_values((k - 6) // UG - 1)
            clear_all()

        turn(-1, units=False, head=True, tail=False)
        turn(0, units=True, head=True, tail=False)
        with nc.Fori(1, B - 1) as b:
            turn(b, units=True, head=True, tail=True)
        turn(B - 1, units=True, head=False, tail=True)
        turn(B, units=False, head=False, tail=True)
        actx.close()

        woS = sb("woS", [P, FC, C])
        boB = sb("boB", [P, C])
        gaB = sb("gaB", [P, C])
        beB = sb("beB", [P, C])
        block_row = sb("block_row", [P, BLOCKS], I32)
        block_expert = sb("block_expert", [P, BLOCKS], I32)
        cnt = sb("cnt", [P, E])
        cnt_i = sb("cnt_i", [P, E], I32)
        nblk = sb("nblk", [P, E])
        ends = [sb(f"ends{i}", [P, E]) for i in range(2)]
        cmp = sb("cmp", [P, BLOCKS, E])
        ebf = sb("ebf", [P, BLOCKS])
        stf = sb("stf", [P, BLOCKS])
        pad_f = sb("pad_f", [P, E])
        pad_i = sb("pad_i", [P, E], I32)
        with nc.Block() as block:
            @block.sync
            def _(sp):
                sp.dma_start(woS[:, :, :], wo.rearrange("(f p) c -> p f c", p=P)).then_inc(s_w, 16)
                for dst, src in ((boB, bo), (gaB, gamma), (beB, beta)):
                    sp.dma_start(dst[:, :], src.partition_broadcast(P)).then_inc(s_w, 16)
                sp.wait_ge(s_w, 64)

            @block.vector
            def _(dve):
                n = [0]

                def link(ins):
                    n[0] += 1
                    ins.then_inc(s_dve, 1)
                    dve.wait_ge(s_dve, n[0])

                link(nc.vector.tensor_scalar(pad_f[:, :], base[:, :], iota_p[:, 0:1], None, ALU.add))
                nc.vector.tensor_copy(pad_i[:, :], pad_f[:, :]).then_inc(s_pos, 1)
                link(nc.vector.scalar_tensor_tensor(out=cnt[:, :], in0=base[:, :], scalar=float(P - 1),
                                                    in1=iota_cap[:, :], op0=ALU.add, op1=ALU.subtract))
                link(nc.vector.tensor_copy(cnt_i[:, :], cnt[:, :]))
                link(nc.vector.tensor_scalar(cnt_i[:, :], cnt_i[:, :], 7, None, ALU.logical_shift_right))
                link(nc.vector.tensor_copy(nblk[:, :], cnt_i[:, :]))
                link(nc.vector.tensor_copy(ends[0][:, :], nblk[:, :]))
                a, z, s = 0, 1, 1
                while s < E:
                    nc.vector.tensor_copy(ends[z][:, 0:s], ends[a][:, 0:s])
                    link(nc.vector.tensor_tensor(ends[z][:, s:E], ends[a][:, s:E], ends[a][:, 0:E - s], ALU.add))
                    a, z, s = z, a, 2 * s
                link(nc.vector.tensor_tensor(cmp[:, :, :], bc(ends[a][:, :].unsqueeze(1), [P, BLOCKS, E]),
                                             bc(iota_k[:, :].unsqueeze(2), [P, BLOCKS, E]), ALU.is_le))
                link(nc.vector.reduce_sum(ebf[:, :], cmp[:, :, :], AXX))
                link(nc.vector.tensor_tensor(cmp[:, :, :], cmp[:, :, :],
                                             bc(nblk[:, :].unsqueeze(1), [P, BLOCKS, E]), ALU.mult))
                link(nc.vector.reduce_sum(stf[:, :], cmp[:, :, :], AXX))
                link(nc.vector.tensor_tensor(stf[:, :], iota_k[:, :], stf[:, :], ALU.subtract))
                link(nc.vector.scalar_tensor_tensor(out=stf[:, :], in0=ebf[:, :], scalar=float(E), in1=stf[:, :],
                                                    op0=ALU.is_lt, op1=ALU.mult))
                link(nc.vector.scalar_tensor_tensor(out=stf[:, :], in0=ebf[:, :], scalar=float(CAPB), in1=stf[:, :],
                                                    op0=ALU.mult, op1=ALU.add))
                nc.vector.tensor_copy(block_row[:, :], stf[:, :])
                link(nc.vector.tensor_scalar(ebf[:, :], ebf[:, :], float(E - 1), None, ALU.min))
                link(nc.vector.tensor_copy(block_expert[:, :], ebf[:, :]))

            @block.gpsimd
            def _(pool):
                pool.wait_ge(s_pos, 1)
                for e in range(E):
                    pool.indirect_dma_start(out=xs_d, out_offset=bass.IndirectOffsetOnAxis(ap=pad_i[:, e:e + 1], axis=0),
                                            in_=fill[:, :], in_offset=None).then_inc(s_pad, 16)
                pool.wait_ge(s_pad, 16 * E)
        clear_all()

        w1_v = w1.rearrange("e (c p) f -> e p c f", p=P)
        b1_v = b1.rearrange("e (f p) -> e p f", p=P)
        xs_v = xs_d.rearrange("(k p) c -> k p c", p=P)
        out_v = out.rearrange("b t c -> (b t) c")
        NG = PER_ITER // BG
        rows = [sb(f"rows{i}", [P, ROW]) for i in range(RR)]
        hb = [sb(f"hb{i}", [P, C]) for i in range(RR)]
        w1S = [sb(f"w1S{i}", [P, CC, FF]) for i in range(RW)]
        b1S = [sb(f"b1S{i}", [P, FC]) for i in range(RW)]
        hnT = [sb(f"hnT{i}", [P, CC, P]) for i in range(2)]
        hid = [sb(f"hid{i}", [P, FC, P]) for i in range(2)]
        acc = [sb(f"acc{i}", [P, BG, C]) for i in range(2)]
        res = [sb(f"res{i}", [P, BG, C]) for i in range(2)]
        ids = [sb(f"ids{i}", [P, BG], I32) for i in range(2)]
        e6 = sb("e6", [P, BG, 6])
        emv = sb("emv", [P, BG, 2])
        ers = sb("ers", [P, BG])
        eva = sb("eva", [P, BG])
        etm = sb("etm", [P, BG])

        with nc.Fori(0, ITERS) as it:
            with nc.Block() as block:
                @block.sync
                def _(sp):
                    for k in range(PER_ITER):
                        i = k % RR
                        if k >= RR:
                            sp.wait_ge(s_res, (k - RR) // BG + 1)
                            sp.wait_ge(s_ehT, k - RR + 1)
                        at = sp.value_load(block_row[0:1, bass.ds(it * PER_ITER + k, 1)], min_val=0, max_val=E * CAPB)
                        sp.dma_start(rows[i][:, :], xs_v[bass.ds(at, 1)].rearrange("o p c -> p (o c)")
                                     ).then_inc(s_rows[i], 16)
                        i = k % RW
                        if k >= RW:
                            sp.wait_ge(s_up, k - RW + 1)
                            sp.wait_ge(s_gelu, 2 * (k - RW + 1))
                        e = sp.value_load(block_expert[0:1, bass.ds(it * PER_ITER + k, 1)], min_val=0, max_val=E - 1)
                        sp.dma_start(w1S[i][:, :, :], w1_v[bass.ds(e, 1)].rearrange("o p c f -> p (o c) f")
                                     ).then_inc(s_w1[i], 16)
                        with nc.allow_non_contiguous_dma("an expert's bias, a column per chunk"):
                            sp.dma_start(b1S[i][:, :], b1_v[bass.ds(e, 1)].rearrange("o p f -> p (o f)")
                                         ).then_inc(s_w1[i], 16)

                @block.vector
                def _(dve):
                    n = [0]

                    def link(ins):
                        n[0] += 1
                        ins.then_inc(s_dve, 1)
                        dve.wait_ge(s_dve, n[0])

                    def normalise(a, eps, signal):
                        for j in range(BG):
                            last = nc.vector.bn_stats(e6[:, j, :], a[:, j, :])
                        link(last)
                        for j in range(BG):
                            last = nc.vector.bn_aggr(emv[:, j, :], e6[:, j, :])
                        link(last)
                        link(nc.vector.tensor_scalar(eva[:, :], emv[:, :, 1], eps, None, ALU.add))
                        inverse_sqrt(nc, link, ers[:, :], eva[:, :], etm[:, :])
                        for j in range(BG):
                            last = nc.vector.tensor_scalar(a[:, j, :], a[:, j, :], emv[:, j, 0:1], ers[:, j:j + 1],
                                                           ALU.subtract, ALU.mult)
                        last.then_inc(signal, 1)

                    def add_down(k):
                        g, j = k // BG, k % BG
                        dve.wait_ge(s_down, k + 1)
                        dve.wait_ge(s_hb, k + 1)
                        if j == 0 and g >= 2:
                            dve.wait_ge(s_res, g - 1)
                        nc.vector.tensor_tensor(acc[g % 2][:, j, :], bank[4 + k % 2][:, 0:C], hb[k % RR][:, :],
                                                ALU.add).then_inc(s_sum, 1)

                    def first_norm(g):
                        dve.wait_ge(s_sum, BG * (g + 1))
                        normalise(acc[g % 2], 1e-12, s_n1)

                    def second_norm(g):
                        dve.wait_ge(s_gb, g + 1)
                        normalise(acc[g % 2], 1e-5, s_n2)

                    for k in range(PER_ITER):
                        add_down(k)
                        if k % BG == 1 and k > BG:
                            second_norm(k // BG - 1)
                        if k % BG == BG - 1:
                            first_norm(k // BG)
                    second_norm(NG - 1)

                @block.scalar
                def _(act):
                    def copy_hT(k):
                        act.wait_ge(s_ehT, k + 1)
                        if k >= 2:
                            act.wait_ge(s_up, k - 1)
                        nc.scalar.copy(hnT[k % 2][:, :, :],
                                       bank[6 + k % 2][:, 0:CC * P].rearrange("p (c q) -> p c q", c=CC)
                                       ).then_inc(s_ehTc, 1)

                    def gelu(k):
                        i = k % RW
                        act.wait_ge(s_w1[i], 32 * (k // RW + 1))
                        if k >= 2:
                            act.wait_ge(s_down, k - 1)
                        for half in range(2):
                            act.wait_ge(s_up, k + 1)
                            for f in range(half * FC // 2, (half + 1) * FC // 2):
                                at = 1024 * (k % 2) + P * f
                                last = nc.scalar.activation(hid[k % 2][:, f, :], PSH[:, at:at + P], ACT.Gelu,
                                                            bias=b1S[i][:, f:f + 1])
                            last.then_inc(s_gelu, 1)

                    copy_hT(0)
                    for k in range(PER_ITER):
                        if k + 1 < PER_ITER:
                            copy_hT(k + 1)
                        gelu(k)

                @block.tensor
                def _(pe):
                    def turn_rows(k):
                        i = k % RR
                        pe.wait_ge(s_rows[i], 16 * (k // RR + 1))
                        if k >= 2:
                            pe.wait_ge(s_ehTc, k - 1)
                        for c in range(CC):
                            last = nc.tensor.transpose(bank[6 + k % 2][:, c * P:(c + 1) * P],
                                                       rows[i][:, C + c * P:C + (c + 1) * P], ident[:, :])
                        last.then_inc(s_ehT, 1)

                    def up(k):
                        i = k % RW
                        pe.wait_ge(s_ehTc, k + 1)
                        pe.wait_ge(s_w1[i], 32 * (k // RW + 1))
                        if k >= 2:
                            pe.wait_ge(s_gelu, 2 * (k - 1))
                        for f in range(FC):
                            at = 1024 * (k % 2) + P * f
                            for c in range(CC):
                                last = nc.tensor.matmul(PSH[:, at:at + P], w1S[i][:, c, f * P:(f + 1) * P],
                                                        hnT[k % 2][:, c, :], start=(c == 0), stop=(c == CC - 1))
                        last.then_inc(s_up, 1)

                    def down(k):
                        if k >= 2:
                            pe.wait_ge(s_sum, k - 1)
                        for f in range(FC):
                            if f % (FC // 2) == 0:
                                pe.wait_ge(s_gelu, 2 * k + 1 + f // (FC // 2))
                            last = nc.tensor.matmul(bank[4 + k % 2][:, 0:C], hid[k % 2][:, f, :], woS[:, f, :],
                                                    start=(f == 0), stop=(f == FC - 1))
                        last.then_inc(s_down, 1)

                    turn_rows(0)
                    turn_rows(1)
                    up(0)
                    for k in range(PER_ITER):
                        if k + 2 < PER_ITER:
                            turn_rows(k + 2)
                        if k + 1 < PER_ITER:
                            up(k + 1)
                        down(k)

                @block.gpsimd
                def _(pool):
                    n = [0]

                    def link(ins):
                        n[0] += 1
                        ins.then_inc(s_pool, 1)
                        pool.wait_ge(s_pool, n[0])

                    def add_bias(k):
                        pool.wait_ge(s_rows[k % RR], 16 * (k // RR + 1))
                        if k >= RR:
                            pool.wait_ge(s_sum, k - RR + 1)
                        nc.gpsimd.tensor_tensor(hb[k % RR][:, :], rows[k % RR][:, C:2 * C], boB[:, :],
                                                ALU.add).then_inc(s_hb, 1)

                    def gamma_beta(g):
                        a = acc[g % 2][:, :, :]
                        pool.wait_ge(s_n1, g + 1)
                        link(nc.gpsimd.tensor_tensor(a, a, bc(gaB[:, :].unsqueeze(1), [P, BG, C]), ALU.mult))
                        nc.gpsimd.tensor_tensor(a, a, bc(beB[:, :].unsqueeze(1), [P, BG, C]), ALU.add).then_inc(s_gb, 1)

                    def send(g):
                        pool.wait_ge(s_n2, g + 1)
                        if g >= 2:
                            pool.wait_ge(s_out[g % 2], it * (16 * BG * ((NG + 1 - g % 2) // 2)) + 16 * BG * (g // 2))
                        for j in range(BG):
                            r = rows[(g * BG + j) % RR]
                            nc.gpsimd.tensor_tensor(res[g % 2][:, j, :], acc[g % 2][:, j, :], r[:, 0:C], ALU.add)
                        for j in range(BG):
                            r = rows[(g * BG + j) % RR]
                            last = nc.gpsimd.tensor_copy(ids[g % 2][:, j:j + 1], r[:, 2 * C:ROW].bitcast(I32))
                        last.then_inc(s_res, 1)
                        pool.wait_ge(s_res, g + 1)
                        for j in range(BG):
                            pool.indirect_dma_start(
                                out=out_v, out_offset=bass.IndirectOffsetOnAxis(ap=ids[g % 2][:, j:j + 1], axis=0),
                                in_=res[g % 2][:, j, :], in_offset=None, bounds_check=TOK - 1,
                                oob_is_err=False).then_inc(s_out[g % 2], 16)

                    for k in range(min(RR, PER_ITER)):
                        add_bias(k)
                    for g in range(NG):
                        gamma_beta(g)
                        send(g)
                        for k in range(RR + g * BG, min(RR + (g + 1) * BG, PER_ITER)):
                            add_bias(k)
                    for i in range(2):
                        share = (NG + 1 - i) // 2
                        pool.wait_ge(s_out[i], it * (16 * BG * share) + 16 * BG * share)
            clear_all()


def kernel(**inputs):
    import numpy as _np
    import concourse.bacc as _bacc
    from concourse import mybir as _mybir
    from concourse.bass_utils import run_bass_kernel_spmd as _run

    a = {k: _np.asarray(v) for k, v in inputs.items()}
    tr = lambda m: _np.ascontiguousarray(_np.swapaxes(m, -1, -2))
    laid = [
        ("x", a["L0_attn_x"]),
        ("w_all", _np.ascontiguousarray(_np.concatenate(
            [tr(a["L0_attn_Wqkv"]), tr(a["L0_attn_Walpha"]), tr(a["L0_attn_Wimp"])], axis=1))),
        ("b_all", _np.concatenate([a["L0_attn_bqkv"], a["L0_attn_balpha"], a["L0_attn_bimp"]])),
        ("wout_t", tr(a["L0_attn_Wout"])),
        ("bout", a["L0_attn_bout"]),
        ("thr", a["L0_attn_spike_threshold"].reshape(1)),
        ("log_k", a["L0_attn_log_k"]),
        ("qk_scale", a["L0_attn_qk_scale"].reshape(1)),
        ("wr_t", tr(a["L0_ffn_Wr"])),
        ("w1", a["L0_ffn_W1"]),
        ("b1", a["L0_ffn_b1"]),
        ("wo", a["L0_ffn_Wo"]),
        ("bo", a["L0_ffn_bo"]),
        ("gamma", a["L0_ffn_gamma"]),
        ("beta", a["L0_ffn_beta"]),
    ]
    nc = _bacc.Bacc("TRN2", target_bir_lowering=False, num_devices=1)
    arrays, args = {}, []
    for name, v in laid:
        v = _np.ascontiguousarray(v)
        arrays[f"in_{name}"] = v
        args.append(nc.dram_tensor(f"in_{name}", v.shape, _mybir.dt.from_np(v.dtype), kind="ExternalInput").ap())
    args.append(nc.dram_tensor("out_x", (B, T, C), F32, kind="ExternalOutput").ap())
    sandwich_kernel(nc, *args)
    r = _run(nc, [arrays], core_ids=[0])
    return r.results[0]["out_x"]
```

```python
import numpy as np
import concourse.bass as bass
from concourse import mybir
from contextlib import ExitStack

F32 = mybir.dt.float32
BF16 = mybir.dt.bfloat16
I32 = mybir.dt.int32
U32 = mybir.dt.uint32
ALU = mybir.AluOpType
ACT = mybir.ActivationFunctionType
AXX = mybir.AxisListType.X

P = 128
B, T, C = 8, 512, 256
H, D = 16, 16
E, FF = 8, 1024
NT = T // P
CC = C // P
FC = FF // P
TOK = B * T
TILES = TOK // P
HG = 4
G = H // HG
QKV = 3 * C
COLS = QKV + H + 1
NQK = 2 * H
SLOTS = TOK // P + E - 1
BG = 5
NB = 2 * BG
TURNS = -(-SLOTS // NB)
BLOCKS = TURNS * NB
CAPB = TOK // P + 1
ROW = 2 * C + 1
RW = BG
MASKED = -1e30

FA = 2.5069359320797613
FS = 0.02068334648608328
FB = -2.952890362403119
FC0 = 17.482113414249277
FSCALE = 0.42046220252761046
YMIN = float(np.log1p(0.5e-6))
SINH = [1.0 / 6, 1.0 / 120, 1.0 / 5040, 1.0 / 362880, 1.0 / 39916800, 1.0 / 6227020800]


def inverse_sqrt_guess(nc, link, out, v, t):
    link(nc.vector.tensor_scalar(t.bitcast(I32), v.bitcast(I32), 1, None, ALU.logical_shift_right))
    link(nc.vector.tensor_scalar(out.bitcast(I32), t.bitcast(I32), -1.0, float(0x5F3759DF), ALU.mult, ALU.add))


def inverse_sqrt_step(nc, link, out, v, t):
    link(nc.vector.scalar_tensor_tensor(out=t, in0=v, scalar=-0.5, in1=out, op0=ALU.mult, op1=ALU.mult))
    link(nc.vector.tensor_tensor(t, t, out, ALU.mult))
    link(nc.vector.scalar_tensor_tensor(out=out, in0=t, scalar=1.5, in1=out, op0=ALU.add, op1=ALU.mult))


def inverse_sqrt(nc, link, out, v, t):
    inverse_sqrt_guess(nc, link, out, v, t)
    for _ in range(3):
        inverse_sqrt_step(nc, link, out, v, t)


def units_of_group():
    out = []
    for h in (0, 2):
        for k in (h, h + 1):
            out.append([(k, 0, 0, P), (k, 2, P, 3 * P)])
            out.append([(k, 3, 0, 4 * P)])
        out.append([(h, 1, 0, 2 * P), (h + 1, 1, 2 * P, 2 * P)])
    return out


UNITS = [(g, u) for g in range(G) for u in units_of_group()]
UG = len(UNITS) // G
NU = len(UNITS)


def sandwich_kernel(nc, x, w_all, b_all, wout_t, bout, thr, log_k, qk_scale, wr_t, w1, b1, wo, bo, gamma, beta, out):
    ctx = ExitStack()
    with ctx:
        def sb(name, shape, dt=F32):
            return ctx.enter_context(nc.sbuf_tensor(name, shape, dt))

        s_sent = ctx.enter_context(nc.semaphore("rows_sent"))
        s_pad = ctx.enter_context(nc.semaphore("empty_rows_sent"))
        s_out = ctx.enter_context(nc.semaphore("rows_out"))

        cleared = []

        def sem(name):
            s = ctx.enter_context(nc.semaphore(name))
            cleared.append(s.num)
            return s

        def clear_all():
            assert cleared == list(range(cleared[0], cleared[0] + len(cleared)))
            nc.all_engine_barrier(sems_to_clear=range(cleared[0], cleared[-1] + 1))

        def bc(ap, shape):
            return ap.broadcast_to(shape)

        PSH = ctx.enter_context(nc.psum_tensor("banks", [P, 8 * 512], F32))
        bank = [PSH[:, 512 * i:512 * (i + 1)] for i in range(8)]
        MB, EB, PTB = (0, 1), (2, 3), (4, 5)
        BA, BB = 6, 7

        ident = sb("ident", [P, P])
        ident_bf = sb("ident_bf", [P, P], BF16)
        mask_bf = sb("mask_bf", [P, P], BF16)
        ones = sb("ones", [P, P])
        lower = sb("lower", [P, P])
        wall = sb("wall", [P, CC, COLS])
        ball = sb("ball", [P, COLS])
        woutT = sb("woutT", [P, CC, C])
        boutB = sb("boutB", [P, C])
        wrT = sb("wrT", [P, CC, E])
        thrB = sb("thrB", [P, 1])
        logk = sb("logk", [P, H])
        lk2 = sb("lk2", [P, H])
        gcoef = sb("gcoef", [P, H])
        qks = sb("qks", [P, 1])
        safe = sb("safe", [P, 1])
        iota_i = sb("iota_i", [P, 64], I32)
        iota_e = sb("iota_e", [P, E])
        iota_k = sb("iota_k", [P, BLOCKS])
        iota_cap = sb("iota_cap", [P, E])
        cap_i = sb("cap_i", [P, E], I32)
        fill = sb("fill", [P, ROW])

        base = sb("base", [P, E])
        idcol = sb("idcol", [P, NT], I32)

        xs_d = nc.dram_tensor("xs_scratch", ((E * CAPB + 1) * P, ROW), F32, kind="Internal").ap()

        s_w = sem("weights_loaded")
        s_fillset = sem("empty_row_set")
        s_fill = sem("empty_block_stored")
        s_act = sem("act_chain")
        s_dve = sem("dve_chain")
        s_pool = sem("pool_chain")
        s_x = sem("x_loaded")
        s_xr = sem("x_again_loaded")
        s_xn = sem("x_normalised")
        s_xT = sem("x_transposed")
        s_xnT = sem("xT_copied")
        s_proj = sem("projected")
        s_qkv = sem("qkv_biased")
        s_sq = sem("squares_ready")
        s_ez = sem("gate_exp_ready")
        s_var = sem("variances_ready")
        s_guess = sem("inverse_roots_guessed")
        s_tsq = sem("squared_times_ready")
        s_tguess = sem("times_guessed")
        s_ratio = sem("ratios_ready")
        s_stats = sem("times_ready")
        s_tok = sem("operands_built")
        s_v = sem("values_built")
        s_tokT = sem("operands_transposed")
        s_evac = sem("operands_copied")
        s_m = sem("m_ready")
        s_e = sem("e_ready")
        s_ln = sem("y_ready")
        s_a = sem("square1_ready")
        s_b = sem("square2_ready")
        s_d = sem("difference_ready")
        s_t = sem("factor_ready")
        s_f = sem("f_ready")
        s_comb = sem("scores_ready")
        s_ga = sem("gates_copied")
        s_p = sem("probs_ready")
        s_pt = sem("probs_transposed")
        s_ptc = sem("probsT_copied")
        s_pv = sem("pv_done")
        s_ov = sem("pv_copied")
        s_ovT = sem("pv_transposed")
        s_ytok = sem("heads_normalised")
        s_yT = sem("heads_transposed")
        s_yTc = sem("headsT_copied")
        s_o = sem("attention_projected")
        s_on = sem("attention_normalised")
        s_or = sem("attention_read")
        s_x1 = sem("x1_ready")
        s_h = sem("h_normalised")
        s_hT = sem("h_transposed")
        s_hTc = sem("hT_copied")
        s_lg = sem("router_logits_ready")
        s_oh = sem("onehot_ready")
        s_rank = sem("ranks_ready")
        s_pos = sem("slots_ready")
        s_id = sem("numbers_ready")
        s_tab = sem("block_table_ready")
        s_hb = sem("expert_h_biased")
        s_ehT = sem("expert_h_transposed")
        s_ehTc = sem("expert_hT_copied")
        s_up = sem("expert_up_ready")
        s_gelu = sem("gelu_ready")
        s_down = sem("expert_down_ready")
        s_sum = sem("down_read")
        s_res = sem("expert_rows_ready")
        s_hrow = [sem(f"expert_h_loaded_{i}") for i in range(RW)]
        s_rows = [sem(f"rows_loaded_{i}") for i in range(NB)]
        s_w1 = [sem(f"expert_loaded_{i}") for i in range(RW)]

        x_v = x.rearrange("b (t p) c -> b p t c", p=P)

        def batch_of(b):
            one = x_v[b:b + 1] if isinstance(b, int) else x_v[bass.ds(b, 1)]
            return one.rearrange("o p t c -> p (o t) c")

        actx = ExitStack()

        def ab(name, shape, dt=F32):
            return actx.enter_context(nc.sbuf_tensor(name, shape, dt))

        x_sb = ab("x_sb", [P, NT, C])
        xnT = ab("xnT", [P, CC, T])
        xnT2 = ab("xnT2", [P, CC, T])
        st6 = ab("st6", [P, NT, 6])
        mv = ab("mv", [P, NT, 2])
        rstd = ab("rstd", [P, NT])
        vare = ab("vare", [P, NT])
        rtmp = ab("rtmp", [P, NT])
        qkv = ab("qkv", [P, NT, COLS])
        sqb = ab("sqb", [P, NT, NQK, D])
        ez = ab("ez", [P, NT, H + 1])
        spike = ab("spike", [P, NT])
        spike_next = ab("spike_next", [P, NT])
        ga = ab("ga", [P, NT, H])
        ga_next = ab("ga_next", [P, NT, H])
        be = ab("be", [P, NT, H])
        small = [ab(f"small{i}", [P, NT, NQK]) for i in range(7)]
        ratio = ab("ratio", [P, NT, NQK])
        time_ = ab("time_", [P, NT, NQK])
        gaF = ab("gaF", [P, NT, H])
        tokQ = [ab(f"tokQ{i}", [P, NT, HG, 2 * D]) for i in range(2)]
        tokE = [ab(f"tokE{i}", [P, NT, HG, 2 * D]) for i in range(2)]
        tokM = [ab(f"tokM{i}", [P, NT, HG, 2 * D]) for i in range(2)]
        vaug = [ab(f"vaug{i}", [P, NT, HG, 2 * D]) for i in range(G)]
        Qz = [ab(f"Qz{i}", [P, HG, T]) for i in range(2)]
        KE = [ab(f"KE{i}", [P, T]) for i in range(2)]
        KM = [ab(f"KM{i}", [P, T]) for i in range(2)]
        RY, RC = 8, 10
        yR = [ab(f"yR{i}", [P, 512]) for i in range(RY)]
        cR = [ab(f"cR{i}", [P, 512]) for i in range(RC)]
        nm = ab("nm", [P, RC, 2])
        PT = [ab(f"PT{i}", [P, HG, NT * (NT + 1) // 2, P]) for i in range(2)]
        ov = ab("ov", [P, T])
        rs = ab("rs", [P, NT, HG])
        ytok = ab("ytok", [P, NT, C])
        ob = ab("ob", [P, NT, C])
        xrow = ab("xrow", [P, NT, ROW])
        lgs = ab("lgs", [P, NT, E])
        mx8 = ab("mx8", [P, NT, 8])
        ix8 = ab("ix8", [P, NT, 8], U32)
        exf = ab("exf", [P, NT])
        onehot = ab("onehot", [P, NT, E])
        run = ab("run", [P, NT, E])
        posf = ab("posf", [P, NT])
        pos = ab("pos", [P, NT], I32)

        NW = 16 * (3 * CC + 6)
        with nc.Block() as block:
            @block.sync
            def _(sp):
                sp.dma_start(x_sb[:, :, :], batch_of(0)).then_inc(s_w, 16)
                for c in range(CC):
                    sp.dma_start(wall[:, c, :], w_all[c * P:(c + 1) * P, :]).then_inc(s_w, 16)
                    sp.dma_start(woutT[:, c, :], wout_t[c * P:(c + 1) * P, :]).then_inc(s_w, 16)
                    sp.dma_start(wrT[:, c, :], wr_t[c * P:(c + 1) * P, :]).then_inc(s_w, 16)
                sp.dma_start(ball[:, :], b_all.partition_broadcast(P)).then_inc(s_w, 16)
                sp.dma_start(boutB[:, :], bout.partition_broadcast(P)).then_inc(s_w, 16)
                sp.dma_start(thrB[:, :], thr.partition_broadcast(P)).then_inc(s_w, 16)
                sp.dma_start(logk[:, :], log_k.partition_broadcast(P)).then_inc(s_w, 16)
                sp.dma_start(qks[:, :], qk_scale.partition_broadcast(P)).then_inc(s_w, 16)
                sp.wait_ge(s_fillset, 1)
                sp.dma_start(xs_d[E * CAPB * P:(E * CAPB + 1) * P, :], fill[:, :]).then_inc(s_fill, 16)
                sp.wait_ge(s_w, NW)
                sp.wait_ge(s_fill, 16)

            @block.gpsimd
            def _(pool):
                n = [0]

                def link(ins):
                    n[0] += 1
                    ins.then_inc(s_pool, 1)
                    pool.wait_ge(s_pool, n[0])

                nc.gpsimd.memset(fill[:, 0:2 * C], 0.0)
                nc.gpsimd.memset(fill[:, 2 * C:ROW].bitcast(I32), TOK).then_inc(s_fillset, 1)
                nc.gpsimd.memset(ones[:, :], 1.0)
                nc.gpsimd.memset(ident[:, :], 0.0)
                nc.gpsimd.memset(ident_bf[:, :], 0.0)
                link(nc.gpsimd.memset(mask_bf[:, :], 0.0))
                nc.gpsimd.affine_select(out=ident[:, :], in_=ident[:, :], compare_op=ALU.not_equal, fill=1.0,
                                        base=0, pattern=[[-1, P]], channel_multiplier=1)
                nc.gpsimd.affine_select(out=ident_bf[:, :], in_=ident_bf[:, :], compare_op=ALU.not_equal, fill=1.0,
                                        base=0, pattern=[[-1, P]], channel_multiplier=1)
                nc.gpsimd.affine_select(out=mask_bf[:, :], in_=mask_bf[:, :], compare_op=ALU.is_ge, fill=MASKED,
                                        base=0, pattern=[[-1, P]], channel_multiplier=1)
                nc.gpsimd.affine_select(out=lower[:, :], in_=ones[:, :], compare_op=ALU.is_gt, fill=0.0,
                                        base=0, pattern=[[1, P]], channel_multiplier=-1)
                nc.gpsimd.iota(idcol[:, :], pattern=[[P, NT]], base=0, channel_multiplier=1)
                nc.gpsimd.iota(cap_i[:, :], pattern=[[CAPB * P, E]], base=0, channel_multiplier=0)
                link(nc.gpsimd.iota(iota_i[:, 0:BLOCKS], pattern=[[1, BLOCKS]], base=0, channel_multiplier=0))
                nc.gpsimd.tensor_copy(iota_k[:, :], iota_i[:, 0:BLOCKS])
                nc.gpsimd.tensor_copy(iota_e[:, :], iota_i[:, 0:E])
                nc.gpsimd.tensor_copy(base[:, :], cap_i[:, :])
                link(nc.gpsimd.tensor_copy(iota_cap[:, :], cap_i[:, :]))

            @block.scalar
            def _(act):
                nc.scalar.preload_act_table_set("natural_log_exp_and_others")
                act.wait_ge(s_w, NW)
                nc.scalar.activation(safe[:, :], qks[:, :], ACT.Exp, scale=-1.0).then_inc(s_act, 1)
                act.wait_ge(s_dve, 2)
                nc.scalar.activation(lk2[:, :], gcoef[:, :], ACT.Exp, scale=-1.0).then_inc(s_act, 1)
                act.wait_ge(s_act, 2)
                nc.scalar.activation(gcoef[:, :], lk2[:, :], ACT.Ln, bias=1.0).then_inc(s_act, 1)

            @block.vector
            def _(dve):
                n = [0]

                def link(ins):
                    n[0] += 1
                    ins.then_inc(s_dve, 1)
                    dve.wait_ge(s_dve, n[0])

                for t in (*tokE, *tokM):
                    nc.vector.memset(t[:, :, :, :], 0.0)
                for i in range(2):
                    nc.vector.memset(Qz[i][:, :, :], 0.0)
                for i in range(G):
                    last = nc.vector.memset(vaug[i][:, :, :, :], 0.0)
                link(last)
                for i in range(G):
                    nc.vector.memset(vaug[i][:, :, :, D:D + 1], 1.0)
                dve.wait_ge(s_w, NW)
                link(nc.vector.scalar_tensor_tensor(out=gcoef[:, :], in0=logk[:, :], scalar=-1.0, in1=logk[:, :],
                                                    op0=ALU.mult, op1=ALU.max))
                dve.wait_ge(s_act, 1)
                link(nc.vector.tensor_scalar(safe[:, :], safe[:, :], 1.0, None, ALU.add))
                link(nc.vector.reciprocal(safe[:, :], safe[:, :]))
                link(nc.vector.tensor_scalar(safe[:, :], safe[:, :], 1.5, None, ALU.mult))
                dve.wait_ge(s_act, 3)
                link(nc.vector.scalar_tensor_tensor(out=lk2[:, :], in0=logk[:, :], scalar=0.0, in1=gcoef[:, :],
                                                    op0=ALU.max, op1=ALU.add))
                link(nc.vector.tensor_scalar(lk2[:, :], lk2[:, :], 1e-6, None, ALU.add))
                link(nc.vector.reciprocal(lk2[:, :], lk2[:, :]))
                link(nc.vector.tensor_scalar(gcoef[:, :], lk2[:, :], -FSCALE, None, ALU.mult))
        clear_all()

        W_LAG = 1
        D_LAG = 2
        T_LAG = 3
        E_LAG = 4
        F_LAG = 4
        S_LAG = 5
        P_LAG = 6
        X_LAG = 7
        K_LAG = 8
        PREP_AT = {6: 1, 15: 2, 25: 3, 36: G}
        PROJECT_AT = {14: 0, 21: 1, 22: 2, 23: 3}
        BUILD_AT = {0: 1, 3: 2, 7: 3, 33: G}

        def turn(b, units, head, tail):
            preps = (list(range(1, G)) if units else []) + ([G] if head else [])
            prev = tail
            proj_bank = [BA if units else 2 * ((j + NT - 1) % NT) for j in range(NT)]
            HEAD_NORM, TAIL_NORM, TAIL_NORM2 = 1, 1 + head, 2 + head

            def now(k, lag):
                return units if k >= lag else prev

            def done(u, lag):
                if u < 0 and not prev:
                    return 0
                return max(u + lag + 1, 0) if prev else u + 1

            def finished(g):
                return g + 1 + (1 if prev else 0)

            def heads_done(g):
                return g + 1 + (2 if prev else 0)

            def unit_of(k):
                g, unit = UNITS[k % NU]
                return g, unit

            with nc.Block() as block:
                @block.sync
                def _(sp):
                    if head and units:
                        sp.dma_start(x_sb[:, :, :], batch_of(b + 1)).then_inc(s_x, 16)
                    if tail:
                        sp.dma_start(xrow[:, :, 0:C], batch_of(b - 1)).then_inc(s_xr, 16)

                @block.vector
                def _(dve):
                    n = [0]

                    def link(ins):
                        n[0] += 1
                        ins.then_inc(s_dve, 1)
                        dve.wait_ge(s_dve, n[0])

                    def row_stats(rows_of):
                        for j in range(NT):
                            last = nc.vector.bn_stats(st6[:, j, :], rows_of(j))
                        link(last)
                        for j in range(NT):
                            last = nc.vector.bn_aggr(mv[:, j, :], st6[:, j, :])
                        link(last)
                        nc.vector.tensor_scalar(vare[:, :], mv[:, :, 1], 1e-5, None, ALU.add).then_inc(s_var, 1)

                    def row_scale(norm):
                        dve.wait_ge(s_guess, norm)
                        inverse_sqrt_step(nc, link, rstd[:, :], vare[:, :], rtmp[:, :])

                    def normalise(dst_of, rows_of, signal):
                        for j in range(NT):
                            last = nc.vector.tensor_scalar(dst_of(j), rows_of(j), mv[:, j, 0:1], rstd[:, j:j + 1],
                                                           ALU.subtract, ALU.mult)
                        last.then_inc(signal, 1)

                    def distance(u):
                        if done(u, T_LAG) > 0:
                            dve.wait_ge(s_t, done(u, T_LAG))
                        nc.vector.scalar_tensor_tensor(out=cR[u % RC][:, :], in0=yR[u % RY][:, :], scalar=YMIN,
                                                       in1=cR[u % RC][:, :], op0=ALU.max, op1=ALU.mult).then_inc(s_f, 1)

                    def scores(u):
                        dve.wait_ge(s_f, done(u, F_LAG))
                        if done(u, E_LAG) > 0:
                            dve.wait_ge(s_e, done(u, E_LAG))
                        for i, (h, t, off, w) in enumerate(unit_of(u)[1]):
                            last = nc.vector.tensor_tensor_reduce(
                                out=cR[u % RC][:, off:off + w], in0=cR[u % RC][:, off:off + w],
                                in1=bank[EB[u % 2]][:, off:off + w], scale=-1.0, scalar=3e38, op0=ALU.add,
                                op1=ALU.min, accum_out=nm[:, u % RC, i:i + 1])
                        last.then_inc(s_comb, 1)

                    def keep_probsT(u):
                        g, unit = unit_of(u)
                        if done(u, X_LAG) > 0:
                            dve.wait_ge(s_pt, done(u, X_LAG))
                        if u >= UG and u % UG == 0 and finished(g - 2) > 0:
                            dve.wait_ge(s_pv, finished(g - 2))
                        src = bank[PTB[u % 2]]
                        if len(unit) == 2 and unit[0][1] == 1:
                            h = unit[0][0]
                            last = nc.vector.tensor_copy(PT[g % 2][:, h:h + 2, 1:3, :],
                                                         src.rearrange("p (h j q) -> p h j q", h=2, j=2))
                        else:
                            for h, t, off, w in unit:
                                at = t * (t + 1) // 2
                                last = nc.vector.tensor_copy(PT[g % 2][:, h, at:at + t + 1, :],
                                                             src[:, off:off + w].rearrange("p (j q) -> p j q", q=P))
                        last.then_inc(s_ptc, 1)

                    def heads(g):
                        if finished(g) > 0:
                            dve.wait_ge(s_ovT, finished(g))
                        if g == 0 and tail:
                            dve.wait_ge(s_yT, CC)
                        v = bank[BA].rearrange("p (t h d) -> p t h d", t=NT, h=HG)
                        link(nc.vector.reciprocal(rs[:, :, :], v[:, :, :, D]))
                        link(nc.vector.tensor_tensor(rs[:, :, :], rs[:, :, :],
                                                     bc(spike[:, :].unsqueeze(2), [P, NT, HG]), ALU.mult))
                        c = g % G * HG * D
                        dst = ytok[:, :, c:c + HG * D].rearrange("p t (h d) -> p t h d", h=HG)
                        nc.vector.tensor_tensor(dst, v[:, :, :, 0:D], bc(rs[:, :, :].unsqueeze(3), [P, NT, HG, D]),
                                                ALU.mult).then_inc(s_ytok, 1)

                    ob_of = lambda j: ob[:, j, :]
                    x1_of = lambda j: xrow[:, j, 0:C]
                    h_of = lambda j: xrow[:, j, C:2 * C]

                    def tail_bias():
                        dve.wait_ge(s_o, NT)
                        nc.vector.tensor_tensor(ob[:, :, :], PSH[:, 512 * BA:512 * (BA + 2)].rearrange(
                            "p (t c) -> p t c", t=NT), bc(boutB[:, :].unsqueeze(1), [P, NT, C]),
                            ALU.add).then_inc(s_or, 1)

                    def tail_stats():
                        dve.wait_ge(s_or, 1)
                        row_stats(ob_of)

                    def tail_norm():
                        row_scale(TAIL_NORM)
                        normalise(ob_of, ob_of, s_on)

                    def tail_norm2():
                        dve.wait_ge(s_x1, 1)
                        row_stats(x1_of)

                    def tail_h():
                        row_scale(TAIL_NORM2)
                        normalise(h_of, x1_of, s_h)

                    def tail_route():
                        dve.wait_ge(s_lg, 1)
                        link(nc.vector.tensor_copy(lgs[:, :, :],
                                                   bank[BA][:, 0:NT * E].rearrange("p (t e) -> p t e", t=NT)))
                        for j in range(NT):
                            last = nc.vector.max(mx8[:, j, :], lgs[:, j, :])
                        link(last)
                        for j in range(NT):
                            last = nc.vector.max_index(ix8[:, j, :], mx8[:, j, :], lgs[:, j, :])
                        link(last)
                        link(nc.vector.tensor_copy(exf[:, :], ix8[:, :, 0]))
                        nc.vector.tensor_tensor(onehot[:, :, :], bc(exf[:, :].unsqueeze(2), [P, NT, E]),
                                                bc(iota_e[:, :].unsqueeze(1), [P, NT, E]), ALU.is_equal
                                                ).then_inc(s_oh, 1)

                    def tail_slots():
                        dve.wait_ge(s_rank, 1)
                        rank = bank[BA][:, 64:64 + NT * E].rearrange("p (t e) -> p t e", t=NT)
                        tot = bank[BA][:, 128:128 + NT * E].rearrange("p (t e) -> p t e", t=NT)
                        link(nc.vector.tensor_copy(run[:, 0, :], base[:, :]))
                        for j in range(1, NT):
                            link(nc.vector.tensor_tensor(run[:, j, :], run[:, j - 1, :], tot[:, j - 1, :], ALU.add))
                        link(nc.vector.tensor_tensor(base[:, :], run[:, NT - 1, :], tot[:, NT - 1, :], ALU.add))
                        link(nc.vector.tensor_tensor(run[:, :, :], run[:, :, :], rank, ALU.add))
                        link(nc.vector.tensor_tensor(run[:, :, :], run[:, :, :], onehot[:, :, :], ALU.mult))
                        link(nc.vector.reduce_sum(posf[:, :], run[:, :, :], AXX))
                        nc.vector.tensor_copy(pos[:, :], posf[:, :]).then_inc(s_pos, 1)
                        dve.wait_ge(s_id, 1)
                        nc.vector.tensor_scalar(idcol[:, :], idcol[:, :], float(T), None, ALU.add)

                    x_of = lambda j: x_sb[:, j, :]

                    def head_stats():
                        if units:
                            dve.wait_ge(s_x, 16)
                        row_stats(x_of)

                    def head_norm():
                        row_scale(HEAD_NORM)
                        normalise(x_of, x_of, s_xn)

                    def head_bias(j):
                        dve.wait_ge(s_proj, j + 1)
                        if units and j == 0:
                            dve.wait_ge(s_tok, 6 * (G - 1))
                            dve.wait_ge(s_v, G - 1)
                        nc.vector.tensor_tensor(qkv[:, j, :], PSH[:, 512 * proj_bank[j]:512 * proj_bank[j] + COLS],
                                                ball[:, :], ALU.add).then_inc(s_qkv, 1)

                    def head_gates():
                        dve.wait_ge(s_ez, 1)
                        link(nc.vector.tensor_scalar(ez[:, :, :], ez[:, :, :], 1.0, None, ALU.add))
                        link(nc.vector.reciprocal(ez[:, :, :], ez[:, :, :]))
                        if units:
                            dve.wait_ge(s_ga, 1)
                        nc.vector.tensor_scalar(spike_next[:, :], ez[:, :, H], thrB[:, 0:1], None, ALU.is_gt)
                        nc.vector.tensor_tensor(ga_next[:, :, :], ez[:, :, 0:H],
                                                bc(gcoef[:, :].unsqueeze(1), [P, NT, H]), ALU.mult)
                        nc.vector.tensor_scalar(be[:, :, :], ez[:, :, 0:H], -0.25, 0.25, ALU.mult, ALU.add)

                    ss, inv, i2, z, r, sp2, t2 = [s[:, :, :] for s in small]
                    q0 = sqb[:, :, :, 0]

                    def head_sums(j):
                        dve.wait_ge(s_sq, j + 1)
                        link(nc.vector.reduce_sum(ss[:, j, :], sqb[:, j, :, :], AXX))

                    def head_squares():
                        nc.vector.tensor_scalar(t2, ss, 1e-24, None, ALU.max)
                        nc.vector.tensor_tensor(sp2, ss, q0, ALU.subtract)
                        link(nc.vector.scalar_tensor_tensor(out=z, in0=q0, scalar=-2.0, in1=ss, op0=ALU.mult,
                                                            op1=ALU.add))
                        inverse_sqrt_guess(nc, link, inv, t2, i2)

                    def head_inverse_norms():
                        inverse_sqrt_step(nc, link, inv, t2, i2)

                    def head_ratios():
                        link(nc.vector.tensor_scalar(inv, inv, safe[:, 0:1], None, ALU.mult))
                        link(nc.vector.tensor_tensor(i2, inv, inv, ALU.mult))
                        link(nc.vector.tensor_tensor(z, z, i2, ALU.mult))
                        link(nc.vector.tensor_scalar(z, z, 1e-8, None, ALU.max))

                    def head_ratios2(start, end):
                        for i in range(start, end):
                            c = SINH[len(SINH) - 1 - i]
                            if i == 0:
                                link(nc.vector.tensor_scalar(r, z, c, None, ALU.mult))
                            else:
                                link(nc.vector.scalar_tensor_tensor(out=r, in0=r, scalar=c, in1=z, op0=ALU.add,
                                                                    op1=ALU.mult))
                        if end == len(SINH):
                            link(nc.vector.scalar_tensor_tensor(out=r, in0=r, scalar=1.0, in1=inv, op0=ALU.add,
                                                                op1=ALU.mult))

                    def head_times():
                        link(nc.vector.tensor_tensor(t2, r, r, ALU.mult))
                        nc.vector.tensor_copy(ratio[:, :, 0:H], r[:, :, 0:H])
                        nc.vector.tensor_scalar(ratio[:, :, H:NQK], r[:, :, H:NQK], -1.0, None,
                                                ALU.mult).then_inc(s_ratio, 1)
                        link(nc.vector.tensor_tensor(t2, t2, sp2, ALU.mult))
                        nc.vector.tensor_scalar(t2, t2, 1.0, None, ALU.add).then_inc(s_tsq, 1)

                    def head_times2():
                        dve.wait_ge(s_tguess, 1)
                        inverse_sqrt_step(nc, link, i2, t2, z)
                        nc.vector.tensor_tensor(time_[:, :, :], t2, i2, ALU.mult).then_inc(s_stats, 1)

                    for k in range(NU):
                        if tail and k == 14:
                            tail_bias()
                        if tail and k == 36:
                            tail_slots()
                        if now(k, S_LAG):
                            scores(k - S_LAG)
                        if prev and k == 0:
                            heads(-2)
                        if prev and k == 10:
                            heads(-1)
                        if units and k in (20, 30):
                            heads(k // UG - 2)
                        if now(k, K_LAG):
                            keep_probsT(k - K_LAG)
                        if now(k, F_LAG):
                            distance(k - F_LAG)
                        if head and k - 1 in PROJECT_AT:
                            head_bias(PROJECT_AT[k - 1])
                        if units and k == 11:
                            link(nc.vector.tensor_copy(spike[:, :], spike_next[:, :]))
                        if head and k == 1:
                            head_stats()
                        if head and k == 3:
                            head_norm()
                        if tail and k == 16:
                            tail_stats()
                        if tail and k == 18:
                            tail_norm()
                        if tail and k == 20:
                            tail_norm2()
                        if tail and k == 22:
                            tail_h()
                        if head and k - 3 in PROJECT_AT:
                            head_sums(PROJECT_AT[k - 3])
                        if head and k == 26:
                            head_gates()
                        if head and k == 27:
                            head_squares()
                            head_inverse_norms()
                        if head and k == 28:
                            head_inverse_norms()
                            head_inverse_norms()
                        if head and k == 29:
                            head_ratios()
                        if head and k == 30:
                            head_ratios2(0, 3)
                        if head and k == 31:
                            head_ratios2(3, len(SINH))
                        if head and k == 32:
                            head_times()
                        if tail and k == 34:
                            tail_route()
                        if head and k == 34:
                            head_times2()

                @block.scalar
                def _(act):
                    def copy_operands_qe(g):
                        i, at = g % 2, preps.index(g)
                        if units and done(UG * (g - 1) - 1, E_LAG) > 0:
                            act.wait_ge(s_e, done(UG * (g - 1) - 1, E_LAG))
                        act.wait_ge(s_tokT, 3 * at + 1)
                        for h in range(HG):
                            rows = slice(2 * D * h, 2 * D * (h + 1))
                            last = nc.scalar.copy(Qz[i][rows, h, :], bank[BA][rows, :])
                        last.then_inc(s_evac, 1)
                        act.wait_ge(s_tokT, 3 * at + 2)
                        nc.scalar.copy(KE[i][:, :], bank[BB]).then_inc(s_evac, 1)

                    def copy_operands_m(g):
                        act.wait_ge(s_tokT, 3 * preps.index(g) + 3)
                        nc.scalar.copy(KM[g % 2][:, :], bank[BA]).then_inc(s_evac, 1)

                    def log(u):
                        act.wait_ge(s_m, done(u, 0))
                        if done(u - RY, F_LAG) > 0:
                            act.wait_ge(s_f, done(u - RY, F_LAG))
                        nc.scalar.activation(yR[u % RY][:, :], bank[MB[u % 2]], ACT.Ln, bias=0.5,
                                             scale=0.5).then_inc(s_ln, 1)

                    def square1(u):
                        act.wait_ge(s_ln, done(u, 0))
                        if done(u - RC, X_LAG) > 0:
                            act.wait_ge(s_pt, done(u - RC, X_LAG))
                        nc.scalar.activation(cR[u % RC][:, :], yR[u % RY][:, :], ACT.Square, bias=FA).then_inc(s_a, 1)

                    def square2(u):
                        if done(u, 0) > 0:
                            act.wait_ge(s_a, done(u, 0))
                        nc.scalar.activation(cR[u % RC][:, :], cR[u % RC][:, :], ACT.Square, bias=FB,
                                             scale=FS).then_inc(s_b, 1)

                    def probs(u):
                        if done(u, S_LAG) > 0:
                            act.wait_ge(s_comb, done(u, S_LAG))
                        for i, (h, t, off, w) in enumerate(unit_of(u)[1]):
                            last = nc.scalar.activation(cR[u % RC][:, off:off + w], cR[u % RC][:, off:off + w], ACT.Exp,
                                                        bias=nm[:, u % RC, i:i + 1], scale=-1.0)
                        last.then_inc(s_p, 1)

                    def copy_pv(g):
                        act.wait_ge(s_pv, finished(g))
                        if finished(g) >= 2:
                            act.wait_ge(s_ovT, finished(g) - 1)
                        nc.scalar.copy(ov[:, :], bank[BB]).then_inc(s_ov, 1)

                    def copy_transposed(dst, ready, done_):
                        for c in range(CC):
                            act.wait_ge(ready, c + 1)
                            nc.scalar.copy(dst[:, c, :], bank[BA + c]).then_inc(done_, 1)

                    n = [0]

                    def guess_inverse_sqrt(out, v, signal):
                        n[0] += 1
                        nc.scalar.activation(out, v, ACT.Ln).then_inc(s_act, 1)
                        act.wait_ge(s_act, n[0])
                        nc.scalar.activation(out, out, ACT.Exp, scale=-0.5).then_inc(signal, 1)

                    def guess_row_scale(norm):
                        act.wait_ge(s_var, norm)
                        guess_inverse_sqrt(rstd[:, :], vare[:, :], s_guess)

                    for k in range(NU):
                        if now(k, P_LAG):
                            probs(k - P_LAG)
                        if PREP_AT.get(k - 1) in preps:
                            copy_operands_qe(PREP_AT[k - 1])
                        if PREP_AT.get(k - 2) in preps:
                            copy_operands_m(PREP_AT[k - 2])
                        if now(k, W_LAG):
                            square2(k - W_LAG)
                        if units:
                            log(k)
                        if head and k == 2:
                            guess_row_scale(HEAD_NORM)
                        if tail and k == 17:
                            guess_row_scale(TAIL_NORM)
                        if tail and k == 21:
                            guess_row_scale(TAIL_NORM2)
                        if head and k == 33:
                            act.wait_ge(s_tsq, 1)
                            guess_inverse_sqrt(small[2][:, :, :], small[6][:, :, :], s_tguess)
                        if head and k == 6:
                            copy_transposed(xnT, s_xT, s_xnT)
                        if tail and k == 12:
                            copy_transposed(xnT2, s_yT, s_yTc)
                        if tail and k == 32:
                            copy_transposed(xnT2, s_hT, s_hTc)
                        if head and k == 25:
                            act.wait_ge(s_qkv, NT)
                            nc.scalar.activation(ez[:, :, :], qkv[:, :, QKV:COLS], ACT.Exp,
                                                 scale=-1.0).then_inc(s_ez, 1)
                        if head and k - 2 in PROJECT_AT:
                            j = PROJECT_AT[k - 2]
                            act.wait_ge(s_qkv, j + 1)
                            nc.scalar.activation(sqb[:, j, :, :].rearrange("p n d -> p (n d)"),
                                                 qkv[:, j, 0:2 * C], ACT.Square).then_inc(s_sq, 1)
                        if prev and k == 8:
                            copy_pv(-1)
                        if units and k in (18, 28, 38):
                            copy_pv(k // UG - 1)
                        if units:
                            square1(k)

                @block.gpsimd
                def _(pool):
                    def part(col, g):
                        at = col + g % G * HG * D
                        return qkv[:, :, at:at + HG * D].rearrange("p t (h d) -> p t h d", h=HG)

                    S = [P, NT, HG, D]
                    S1 = [P, NT, HG, D - 1]

                    def build_q(g):
                        hq = slice(g % G * HG, (g % G + 1) * HG)
                        q, dst = part(0, g), tokQ[g % 2]
                        if g == G:
                            pool.wait_ge(s_ratio, 1)
                        if preps.index(g) >= 2:
                            pool.wait_ge(s_tokT, 3 * preps.index(g) - 3)
                        nc.gpsimd.tensor_tensor(dst[:, :, :, 0:D], q, bc(be[:, :, hq].unsqueeze(3), S),
                                                ALU.mult).then_inc(s_tok, 1)
                        nc.gpsimd.tensor_tensor(dst[:, :, :, D + 1:2 * D], q[:, :, :, 1:D],
                                                bc(ratio[:, :, hq].unsqueeze(3), S1), ALU.mult).then_inc(s_tok, 1)

                    def build_k(g):
                        hk = slice(H + g % G * HG, H + (g % G + 1) * HG)
                        kk = part(C, g)
                        nc.gpsimd.tensor_copy(tokE[g % 2][:, :, :, 0:D], kk).then_inc(s_tok, 1)
                        nc.gpsimd.tensor_tensor(tokM[g % 2][:, :, :, D + 1:2 * D], kk[:, :, :, 1:D],
                                                bc(ratio[:, :, hk].unsqueeze(3), S1), ALU.mult).then_inc(s_tok, 1)

                    def build_v(g):
                        hq = slice(g % G * HG, (g % G + 1) * HG)
                        hk = slice(H + g % G * HG, H + (g % G + 1) * HG)
                        if g == G:
                            pool.wait_ge(s_stats, 1)
                        nc.gpsimd.tensor_copy(tokQ[g % 2][:, :, :, D], time_[:, :, hq]).then_inc(s_tok, 1)
                        nc.gpsimd.tensor_copy(tokM[g % 2][:, :, :, D], time_[:, :, hk]).then_inc(s_tok, 1)
                        if g == G - 1 and prev:
                            pool.wait_ge(s_pv, finished(-1))
                        if g == G and units:
                            pool.wait_ge(s_pv, finished(0))
                        nc.gpsimd.tensor_copy(vaug[g % G][:, :, :, 0:D], part(2 * C, g)).then_inc(s_v, 1)

                    def difference(u):
                        if done(u, W_LAG) > 0:
                            pool.wait_ge(s_b, done(u, W_LAG))
                        nc.gpsimd.tensor_tensor(cR[u % RC][:, :], yR[u % RY][:, :], cR[u % RC][:, :],
                                                ALU.subtract).then_inc(s_d, 1)

                    def factor(u):
                        g, unit = unit_of(u)
                        if done(u, D_LAG) > 0:
                            pool.wait_ge(s_d, done(u, D_LAG))
                        for h, t, off, w in unit:
                            head_ = slice(g * HG + h, g * HG + h + 1)
                            last = nc.gpsimd.tensor_scalar(cR[u % RC][:, off:off + w], cR[u % RC][:, off:off + w],
                                                           ga[:, t, head_], gaF[:, t, head_], ALU.mult, ALU.add)
                        last.then_inc(s_t, 1)

                    for k in range(NU):
                        if units and k == T_LAG:
                            if prev:
                                pool.wait_ge(s_t, T_LAG)
                            nc.gpsimd.tensor_copy(ga[:, :, :], ga_next[:, :, :])
                            nc.gpsimd.tensor_scalar(gaF[:, :, :], ga_next[:, :, :], FC0, 0.0, ALU.mult,
                                                    ALU.add).then_inc(s_ga, 1)
                            pool.wait_ge(s_ga, 1)
                        if now(k, T_LAG):
                            factor(k - T_LAG)
                        if now(k, D_LAG):
                            difference(k - D_LAG)
                        if tail and k == 3:
                            nc.gpsimd.tensor_copy(xrow[:, :, 2 * C].bitcast(I32), idcol[:, :]).then_inc(s_id, 1)
                        if tail and k == 19:
                            pool.wait_ge(s_on, 1)
                            pool.wait_ge(s_xr, 16)
                            nc.gpsimd.tensor_tensor(xrow[:, :, 0:C], xrow[:, :, 0:C], ob[:, :, :],
                                                    ALU.add).then_inc(s_x1, 1)
                        if tail and k == 36:
                            pool.wait_ge(s_pos, 1)
                            pool.wait_ge(s_h, 1)
                            pool.wait_ge(s_id, 1)
                            for j in range(NT):
                                pool.indirect_dma_start(
                                    out=xs_d, out_offset=bass.IndirectOffsetOnAxis(ap=pos[:, j:j + 1], axis=0),
                                    in_=xrow[:, j, :], in_offset=None).then_inc(s_sent, 16)
                        for first, build in ((0, build_q), (1, build_k), (2, build_v)):
                            g = BUILD_AT.get(k - first)
                            if g in preps:
                                build(g)
                    if tail:
                        pool.wait_ge(s_sent, b * (16 * NT))

                @block.tensor
                def _(pe):
                    def transpose_into(dst, src):
                        for j in range(NT):
                            last = nc.tensor.transpose(bank[dst][:, j * P:(j + 1) * P],
                                                       src[:, j, :, :].rearrange("p h d -> p (h d)"), ident[:, :])
                        last.then_inc(s_tokT, 1)

                    def transpose_operands_qe(g):
                        at = preps.index(g)
                        pe.wait_ge(s_tok, 6 * (at + 1))
                        if at >= 1:
                            pe.wait_ge(s_evac, 3 * at)
                        if g == 1 and prev:
                            pe.wait_ge(s_ytok, heads_done(-2))
                        if g == 1 and head:
                            pe.wait_ge(s_xnT, CC)
                        if g == 2 and tail:
                            pe.wait_ge(s_or, 1)
                        if g == 2 and head:
                            pe.wait_ge(s_qkv, 1)
                        if g in (3, G) and head:
                            pe.wait_ge(s_qkv, NT)
                        if g >= 3 and units:
                            pe.wait_ge(s_ytok, heads_done(g - 3))
                        if g == G and tail:
                            pe.wait_ge(s_pos, 1)
                        transpose_into(BA, tokQ[g % 2])
                        transpose_into(BB, tokE[g % 2])

                    def transpose_operands_m(g):
                        pe.wait_ge(s_evac, 3 * preps.index(g) + 1)
                        transpose_into(BA, tokM[g % 2])

                    def lorentz(u):
                        g, unit = unit_of(u)
                        if u % UG == 0 and g >= 1:
                            pe.wait_ge(s_evac, 3 * g)
                        if done(u - 2, 0) > 0:
                            pe.wait_ge(s_ln, done(u - 2, 0))
                        for h, t, off, w in unit:
                            last = nc.tensor.matmul(bank[MB[u % 2]][:, off:off + w],
                                                    Qz[g % 2][:, h, t * P:(t + 1) * P], KM[g % 2][:, 0:w],
                                                    start=True, stop=True)
                        last.then_inc(s_m, 1)

                    def dots(u):
                        g, unit = unit_of(u)
                        if done(u - 2, S_LAG) > 0:
                            pe.wait_ge(s_comb, done(u - 2, S_LAG))
                        for h, t, off, w in unit:
                            dst = bank[EB[u % 2]]
                            nc.tensor.matmul(dst[:, off:off + w], Qz[g % 2][:, h, t * P:(t + 1) * P],
                                             KE[g % 2][:, 0:w], start=True, stop=False)
                            last = nc.tensor.matmul(dst[:, off + w - P:off + w], ident_bf[:, :], mask_bf[:, :],
                                                    start=False, stop=True)
                        last.then_inc(s_e, 1)

                    def transpose_probs(u):
                        if done(u, P_LAG) > 0:
                            pe.wait_ge(s_p, done(u, P_LAG))
                        if done(u - 2, K_LAG) > 0:
                            pe.wait_ge(s_ptc, done(u - 2, K_LAG))
                        for j in range(4):
                            last = nc.tensor.transpose(bank[PTB[u % 2]][:, j * P:(j + 1) * P],
                                                       cR[u % RC][:, j * P:(j + 1) * P], ident[:, :])
                        last.then_inc(s_pt, 1)

                    def values(g):
                        if g >= 1:
                            pe.wait_ge(s_v, g)
                        if done(UG * (g + 1) - 1, K_LAG) > 0:
                            pe.wait_ge(s_ptc, done(UG * (g + 1) - 1, K_LAG))
                        if units:
                            pe.wait_ge(s_evac, 3 * (g + 1) + 2 if g + 2 in preps else 3 * len(preps))
                        for t in range(NT):
                            for j in range(t + 1):
                                for h in range(HG):
                                    last = nc.tensor.matmul(bank[BB][2 * D * h:2 * D * (h + 1), t * P:(t + 1) * P],
                                                            vaug[g % G][:, j, h, :],
                                                            PT[g % 2][:, h, t * (t + 1) // 2 + j, :],
                                                            start=(j == 0), stop=(j == t),
                                                            tile_position=(0, 2 * D * h), skip_group_check=True)
                        last.then_inc(s_pv, 1)

                    def transpose_values(g):
                        pe.wait_ge(s_ov, finished(g))
                        if units:
                            pe.wait_ge(s_evac, 3 * (g + 2) if g + 2 in preps else 3 * len(preps))
                        if g == -1:
                            pe.wait_ge(s_ytok, heads_done(-2))
                        if g == 2 and tail:
                            pe.wait_ge(s_pos, 1)
                        for j in range(NT):
                            last = nc.tensor.transpose(bank[BA][:, j * P:(j + 1) * P], ov[:, j * P:(j + 1) * P],
                                                       ident[:, :])
                        last.then_inc(s_ovT, 1)

                    def transpose_rows(rows_of, signal):
                        for c in range(CC):
                            for j in range(NT):
                                last = nc.tensor.transpose(bank[BA + c][:, j * P:(j + 1) * P],
                                                           rows_of(j)[:, c * P:(c + 1) * P], ident[:, :])
                            last.then_inc(signal, 1)

                    def project_out():
                        pe.wait_ge(s_yTc, CC)
                        for j in range(NT):
                            for c in range(CC):
                                last = nc.tensor.matmul(bank[BA + j // 2][:, (j % 2) * C:(j % 2 + 1) * C],
                                                        xnT2[:, c, j * P:(j + 1) * P], woutT[:, c, :],
                                                        start=(c == 0), stop=(c == CC - 1))
                            last.then_inc(s_o, 1)

                    def route():
                        pe.wait_ge(s_hTc, CC)
                        for j in range(NT):
                            for c in range(CC):
                                last = nc.tensor.matmul(bank[BA][:, j * E:(j + 1) * E], xnT2[:, c, j * P:(j + 1) * P],
                                                        wrT[:, c, :], start=(c == 0), stop=(c == CC - 1))
                        last.then_inc(s_lg, 1)

                    def rank():
                        pe.wait_ge(s_oh, 1)
                        oh = onehot[:, :, :].rearrange("p i e -> p (i e)")
                        nc.tensor.matmul(bank[BA][:, 64:64 + NT * E], lower[:, :], oh, start=True, stop=True)
                        nc.tensor.matmul(bank[BA][:, 128:128 + NT * E], ones[:, :], oh, start=True,
                                         stop=True).then_inc(s_rank, 1)

                    def project(j):
                        pe.wait_ge(s_xnT, CC)
                        if j == 0 and tail:
                            pe.wait_ge(s_or, 1)
                        if j == 0 and units:
                            pe.wait_ge(s_evac, 3)
                        if j == 1 and units:
                            pe.wait_ge(s_ytok, heads_done(0))
                        if j >= 1 and units:
                            pe.wait_ge(s_qkv, j)
                        for dst, c0, c1 in ((proj_bank[j], 0, 512), (proj_bank[j] + 1, 512, COLS)):
                            for c in range(CC):
                                last = nc.tensor.matmul(bank[dst][:, 0:c1 - c0], xnT[:, c, j * P:(j + 1) * P],
                                                        wall[:, c, c0:c1], start=(c == 0), stop=(c == CC - 1))
                        last.then_inc(s_proj, 1)

                    for k in range(NU):
                        if units:
                            lorentz(k)
                        if now(k, E_LAG):
                            dots(k - E_LAG)
                        if now(k, X_LAG):
                            transpose_probs(k - X_LAG)
                        if PREP_AT.get(k) in preps:
                            transpose_operands_qe(PREP_AT[k])
                        if PREP_AT.get(k - 1) in preps:
                            transpose_operands_m(PREP_AT[k - 1])
                        if prev and k == 7:
                            values(-1)
                        if prev and k == 9:
                            transpose_values(-1)
                        if units and k in (17, 27, 37):
                            values(k // UG - 1)
                        if units and k in (19, 29, 39):
                            transpose_values(k // UG - 1)
                        if head and k == 5:
                            pe.wait_ge(s_xn, 1)
                            if prev:
                                pe.wait_ge(s_ytok, heads_done(-2))
                            transpose_rows(lambda j: x_sb[:, j, :], s_xT)
                        if tail and k == 11:
                            pe.wait_ge(s_ytok, heads_done(-1))
                            transpose_rows(lambda j: ytok[:, j, :], s_yT)
                        if tail and k == 13:
                            project_out()
                        if head and k in PROJECT_AT:
                            project(PROJECT_AT[k])
                        if tail and k == 31:
                            pe.wait_ge(s_h, 1)
                            if units:
                                pe.wait_ge(s_ytok, heads_done(1))
                            else:
                                pe.wait_ge(s_or, 1)
                            transpose_rows(lambda j: xrow[:, j, C:2 * C], s_hT)
                        if tail and k == 33:
                            route()
                        if tail and k == 35:
                            rank()
            clear_all()

        turn(-1, units=False, head=True, tail=False)
        turn(0, units=True, head=True, tail=False)
        with nc.Fori(1, B - 1) as b:
            turn(b, units=True, head=True, tail=True)
        turn(B - 1, units=True, head=False, tail=True)
        turn(B, units=False, head=False, tail=True)
        actx.close()

        woS = sb("woS", [P, FC, C])
        boB = sb("boB", [P, C])
        gaB = sb("gaB", [P, C])
        beB = sb("beB", [P, C])
        block_row = sb("block_row", [P, BLOCKS], I32)
        block_expert = sb("block_expert", [P, BLOCKS], I32)
        cnt = sb("cnt", [P, E])
        cnt_i = sb("cnt_i", [P, E], I32)
        nblk = sb("nblk", [P, E])
        ends = [sb(f"ends{i}", [P, E]) for i in range(2)]
        cmp = sb("cmp", [P, BLOCKS, E])
        ebf = sb("ebf", [P, BLOCKS])
        stf = sb("stf", [P, BLOCKS])
        pad_i = sb("pad_i", [P, E], I32)
        w1_v = w1.rearrange("e (c p) f -> e p c f", p=P)
        b1_v = b1.rearrange("e (f p) -> e p f", p=P)
        xs_v = xs_d.rearrange("(k p) c -> k p c", p=P)
        out_v = out.rearrange("b t c -> (b t) c")
        hrow = [sb(f"hrow{i}", [P, C]) for i in range(RW)]
        xrows = [sb(f"xrows{i}", [P, C]) for i in range(NB)]
        xids = [sb(f"xids{i}", [P, 1]) for i in range(NB)]
        hb = [sb(f"hb{i}", [P, C]) for i in range(RW)]
        w1S = [sb(f"w1S{i}", [P, CC, FF]) for i in range(RW)]
        b1S = [sb(f"b1S{i}", [P, FC]) for i in range(RW)]
        hnT = [sb(f"hnT{i}", [P, CC, P]) for i in range(2)]
        hid = [sb(f"hid{i}", [P, FC, P]) for i in range(2)]
        acc = [sb(f"acc{i}", [P, BG, C]) for i in range(2)]
        res = [sb(f"res{i}", [P, BG, C]) for i in range(2)]
        ids = [sb(f"ids{i}", [P, BG], I32) for i in range(2)]
        e6 = sb("e6", [P, BG, 6])
        emv = sb("emv", [P, BG, 2])
        ers = sb("ers", [P, BG])
        eva = sb("eva", [P, BG])
        etm = sb("etm", [P, BG])

        ROWS_LAG = 2
        UP_LAG = 3
        DOWN_LAG = 4
        RES_LAG = 3
        NORM_AT = (BG - 1 + DOWN_LAG, NB - 1 + DOWN_LAG)

        def expert_turn(it, units, prev):
            spare = 0 if units else BLOCKS - SLOTS

            def now(k, lag):
                return units if k >= lag else prev and k - lag < -spare

            def done(u, lag):
                if u < 0 and not prev:
                    return 0
                return max(u + lag + 1, 0) if prev else u + 1

            def group_at(k, after):
                for g in range(2):
                    at = NORM_AT[g] + after
                    if at == k and units or at == k + NB and prev:
                        return g
                return None

            def groups_done(g, after, here):
                at = NORM_AT[g] + after
                if at < NB <= NORM_AT[g] + here:
                    return 0
                steps = [NORM_AT[x] + after for x in range(2)]
                return sum(1 for x in steps if x % NB <= at % NB and (prev if x >= NB else units))

            with nc.Block() as block:
                @block.sync
                def _(sp):
                    def load_weights(u):
                        i = u % RW
                        if done(u - RW, UP_LAG) > 0:
                            sp.wait_ge(s_up, done(u - RW, UP_LAG))
                            sp.wait_ge(s_gelu, 2 * done(u - RW, UP_LAG))
                        e = sp.value_load(block_expert[0:1, bass.ds(it * NB + u, 1)], min_val=0, max_val=E - 1)
                        sp.dma_start(w1S[i][:, :, :], w1_v[bass.ds(e, 1)].rearrange("o p c f -> p (o c) f")
                                     ).then_inc(s_w1[i], 16)
                        with nc.allow_non_contiguous_dma("an expert's bias, a column per chunk"):
                            sp.dma_start(b1S[i][:, :], b1_v[bass.ds(e, 1)].rearrange("o p f -> p (o f)")
                                         ).then_inc(s_w1[i], 16)

                    def load_rows(u):
                        i = u % RW
                        if done(u - RW, ROWS_LAG) > 0:
                            sp.wait_ge(s_ehT, done(u - RW, ROWS_LAG))
                            sp.wait_ge(s_hb, done(u - RW, ROWS_LAG))
                        at = sp.value_load(block_row[0:1, bass.ds(it * NB + u, 1)], min_val=0, max_val=E * CAPB)
                        sp.dma_start(hrow[i][:, :], xs_v[bass.ds(at, 1), :, C:2 * C].rearrange("o p c -> p (o c)")
                                     ).then_inc(s_hrow[i], 16)

                    def load_residual(u):
                        i = u % NB
                        if u >= 0 and prev:
                            sp.wait_ge(s_res, u // BG + 1)
                        at = sp.value_load(block_row[0:1, bass.ds(it * NB + u, 1)], min_val=0, max_val=E * CAPB)
                        sp.dma_start(xrows[i][:, :], xs_v[bass.ds(at, 1), :, 0:C].rearrange("o p c -> p (o c)")
                                     ).then_inc(s_rows[i], 16)
                        with nc.allow_non_contiguous_dma("a number per row"):
                            sp.dma_start(xids[i][:, :], xs_v[bass.ds(at, 1), :, 2 * C:ROW].rearrange("o p c -> p (o c)")
                                         ).then_inc(s_rows[i], 16)

                    if not prev:
                        sp.dma_start(woS[:, :, :], wo.rearrange("(f p) c -> p f c", p=P)).then_inc(s_w, 16)
                        for dst, src in ((boB, bo), (gaB, gamma), (beB, beta)):
                            sp.dma_start(dst[:, :], src.partition_broadcast(P)).then_inc(s_w, 16)
                        sp.wait_ge(s_pos, 1)
                        for e in range(E):
                            at = sp.value_load(pad_i[0:1, e:e + 1], min_val=0, max_val=E * CAPB * P)
                            sp.dma_start(xs_d[bass.ds(at, P), :], fill[:, :]).then_inc(s_pad, 16)
                        sp.wait_ge(s_tab, 1)
                    for k in range(NB):
                        if units:
                            load_weights(k)
                            if not prev and k == 0:
                                sp.wait_ge(s_pad, 16 * E)
                            load_rows(k)
                        if now(k, RES_LAG):
                            load_residual(k - RES_LAG)
                    if units:
                        for i in range(RW):
                            sp.wait_ge(s_hrow[i], 16 * (NB // RW))
                            sp.wait_ge(s_w1[i], 32 * (NB // RW))
                        for i in range(NB - RES_LAG):
                            sp.wait_ge(s_rows[i], 32)

                @block.vector
                def _(dve):
                    n = [0]

                    def link(ins):
                        n[0] += 1
                        ins.then_inc(s_dve, 1)
                        dve.wait_ge(s_dve, n[0])

                    def block_table():
                        nc.vector.tensor_copy(pad_i[:, :], base[:, :]).then_inc(s_pos, 1)
                        link(nc.vector.scalar_tensor_tensor(out=cnt[:, :], in0=base[:, :], scalar=float(P - 1),
                                                            in1=iota_cap[:, :], op0=ALU.add, op1=ALU.subtract))
                        link(nc.vector.tensor_copy(cnt_i[:, :], cnt[:, :]))
                        link(nc.vector.tensor_scalar(cnt_i[:, :], cnt_i[:, :], 7, None, ALU.logical_shift_right))
                        link(nc.vector.tensor_copy(nblk[:, :], cnt_i[:, :]))
                        link(nc.vector.tensor_copy(ends[0][:, :], nblk[:, :]))
                        a, z, s = 0, 1, 1
                        while s < E:
                            nc.vector.tensor_copy(ends[z][:, 0:s], ends[a][:, 0:s])
                            link(nc.vector.tensor_tensor(ends[z][:, s:E], ends[a][:, s:E], ends[a][:, 0:E - s], ALU.add))
                            a, z, s = z, a, 2 * s
                        link(nc.vector.tensor_tensor(cmp[:, :, :], bc(ends[a][:, :].unsqueeze(1), [P, BLOCKS, E]),
                                                     bc(iota_k[:, :].unsqueeze(2), [P, BLOCKS, E]), ALU.is_le))
                        link(nc.vector.reduce_sum(ebf[:, :], cmp[:, :, :], AXX))
                        link(nc.vector.tensor_tensor(cmp[:, :, :], cmp[:, :, :],
                                                     bc(nblk[:, :].unsqueeze(1), [P, BLOCKS, E]), ALU.mult))
                        link(nc.vector.reduce_sum(stf[:, :], cmp[:, :, :], AXX))
                        link(nc.vector.tensor_tensor(stf[:, :], iota_k[:, :], stf[:, :], ALU.subtract))
                        link(nc.vector.scalar_tensor_tensor(out=stf[:, :], in0=ebf[:, :], scalar=float(E), in1=stf[:, :],
                                                            op0=ALU.is_lt, op1=ALU.mult))
                        link(nc.vector.scalar_tensor_tensor(out=stf[:, :], in0=ebf[:, :], scalar=float(CAPB), in1=stf[:, :],
                                                            op0=ALU.mult, op1=ALU.add))
                        nc.vector.tensor_copy(block_row[:, :], stf[:, :])
                        link(nc.vector.tensor_scalar(ebf[:, :], ebf[:, :], float(E - 1), None, ALU.min))
                        nc.vector.tensor_copy(block_expert[:, :], ebf[:, :]).then_inc(s_tab, 1)

                    def normalise(a, eps):
                        for j in range(BG):
                            last = nc.vector.bn_stats(e6[:, j, :], a[:, j, :])
                        link(last)
                        for j in range(BG):
                            last = nc.vector.bn_aggr(emv[:, j, :], e6[:, j, :])
                        link(last)
                        link(nc.vector.tensor_scalar(eva[:, :], emv[:, :, 1], eps, None, ALU.add))
                        inverse_sqrt(nc, link, ers[:, :], eva[:, :], etm[:, :])
                        for j in range(BG):
                            last = nc.vector.tensor_scalar(a[:, j, :], a[:, j, :], emv[:, j, 0:1], ers[:, j:j + 1],
                                                           ALU.subtract, ALU.mult)
                        link(last)

                    def add_down(u):
                        g, j = u % NB // BG, u % BG
                        dve.wait_ge(s_down, done(u, DOWN_LAG))
                        if done(u, ROWS_LAG) > 0:
                            dve.wait_ge(s_hb, done(u, ROWS_LAG))
                        if u >= 0 and j == 0 and prev:
                            dve.wait_ge(s_res, g + 1)
                        nc.vector.tensor_tensor(acc[g][:, j, :], bank[4 + u % 2][:, 0:C], hb[u % RW][:, :],
                                                ALU.add).then_inc(s_sum, 1)

                    def first_norm(g):
                        u = (g + 1) * BG - 1 if NORM_AT[g] < NB else -1 - spare
                        dve.wait_ge(s_sum, done(u, DOWN_LAG))
                        normalise(acc[g], 1e-12)

                    def gamma_beta(g):
                        a = acc[g][:, :, :]
                        link(nc.vector.tensor_tensor(a, a, bc(gaB[:, :].unsqueeze(1), [P, BG, C]), ALU.mult))
                        link(nc.vector.tensor_tensor(a, a, bc(beB[:, :].unsqueeze(1), [P, BG, C]), ALU.add))

                    def second_norm(g):
                        normalise(acc[g], 1e-5)
                        blocks = range(BG - (spare if g == 1 else 0))
                        for j in blocks:
                            i = g * BG + j
                            if i - NB + RES_LAG >= 0:
                                dve.wait_ge(s_rows[i], 32)
                            nc.vector.tensor_tensor(res[g][:, j, :], acc[g][:, j, :], xrows[i][:, :], ALU.add)
                        for j in blocks:
                            last = nc.vector.tensor_copy(ids[g][:, j:j + 1], xids[g * BG + j][:, :].bitcast(I32))
                        last.then_inc(s_res, 1)

                    if not prev:
                        block_table()
                        dve.wait_ge(s_w, 64)
                    for k in range(NB):
                        if now(k, DOWN_LAG):
                            add_down(k - DOWN_LAG)
                        if group_at(k, 0) is not None:
                            first_norm(group_at(k, 0))
                        if group_at(k, 2) is not None:
                            gamma_beta(group_at(k, 2))
                        if group_at(k, 3) is not None:
                            second_norm(group_at(k, 3))

                @block.scalar
                def _(act):
                    def copy_hT(u):
                        act.wait_ge(s_ehT, done(u, ROWS_LAG))
                        if done(u - 2, UP_LAG) > 0:
                            act.wait_ge(s_up, done(u - 2, UP_LAG))
                        nc.scalar.copy(hnT[u % 2][:, :, :],
                                       bank[6 + u % 2][:, 0:CC * P].rearrange("p (c q) -> p c q", c=CC)
                                       ).then_inc(s_ehTc, 1)

                    def gelu(u):
                        i = u % RW
                        act.wait_ge(s_up, done(u, UP_LAG))
                        if u >= 0:
                            act.wait_ge(s_w1[i], 32 * (u // RW + 1))
                        if done(u - 2, DOWN_LAG) > 0:
                            act.wait_ge(s_down, done(u - 2, DOWN_LAG))
                        for half in range(2):
                            for f in range(half * FC // 2, (half + 1) * FC // 2):
                                at = 1024 * (u % 2) + P * f
                                last = nc.scalar.activation(hid[u % 2][:, f, :], PSH[:, at:at + P], ACT.Gelu,
                                                            bias=b1S[i][:, f:f + 1])
                            last.then_inc(s_gelu, 1)

                    for k in range(NB):
                        if now(k, ROWS_LAG):
                            copy_hT(k - ROWS_LAG)
                        if now(k, UP_LAG):
                            gelu(k - UP_LAG)

                @block.tensor
                def _(pe):
                    def turn_rows(u):
                        if u >= 0:
                            pe.wait_ge(s_hrow[u % RW], 16 * (u // RW + 1))
                        if done(u - 2, ROWS_LAG) > 0:
                            pe.wait_ge(s_ehTc, done(u - 2, ROWS_LAG))
                        for c in range(CC):
                            last = nc.tensor.transpose(bank[6 + u % 2][:, c * P:(c + 1) * P],
                                                       hrow[u % RW][:, c * P:(c + 1) * P], ident[:, :])
                        last.then_inc(s_ehT, 1)

                    def up(u):
                        i = u % RW
                        if done(u, ROWS_LAG) > 0:
                            pe.wait_ge(s_ehTc, done(u, ROWS_LAG))
                        if u >= 0:
                            pe.wait_ge(s_w1[i], 32 * (u // RW + 1))
                        if done(u - 2, UP_LAG) > 0:
                            pe.wait_ge(s_gelu, 2 * done(u - 2, UP_LAG))
                        for f in range(FC):
                            at = 1024 * (u % 2) + P * f
                            for c in range(CC):
                                last = nc.tensor.matmul(PSH[:, at:at + P], w1S[i][:, c, f * P:(f + 1) * P],
                                                        hnT[u % 2][:, c, :], start=(c == 0), stop=(c == CC - 1))
                        last.then_inc(s_up, 1)

                    def down(u):
                        if done(u - 2, DOWN_LAG) > 0:
                            pe.wait_ge(s_sum, done(u - 2, DOWN_LAG))
                        if done(u, UP_LAG) > 0:
                            pe.wait_ge(s_gelu, 2 * done(u, UP_LAG))
                        for f in range(FC):
                            last = nc.tensor.matmul(bank[4 + u % 2][:, 0:C], hid[u % 2][:, f, :], woS[:, f, :],
                                                    start=(f == 0), stop=(f == FC - 1))
                        last.then_inc(s_down, 1)

                    if not prev:
                        pe.wait_ge(s_w, 64)
                    for k in range(NB):
                        if now(k, UP_LAG):
                            up(k - UP_LAG)
                        if now(k, ROWS_LAG):
                            turn_rows(k - ROWS_LAG)
                        if now(k, DOWN_LAG):
                            down(k - DOWN_LAG)

                @block.gpsimd
                def _(pool):
                    def add_bias(u):
                        if u >= 0:
                            pool.wait_ge(s_hrow[u % RW], 16 * (u // RW + 1))
                        if done(u - RW, DOWN_LAG) > 0:
                            pool.wait_ge(s_sum, done(u - RW, DOWN_LAG))
                        nc.gpsimd.tensor_tensor(hb[u % RW][:, :], hrow[u % RW][:, :], boB[:, :],
                                                ALU.add).then_inc(s_hb, 1)

                    def rows_out():
                        pool.wait_ge(s_out, it * (16 * NB) - 16 * spare)

                    def send(g):
                        if groups_done(g, 3, 4) > 0:
                            pool.wait_ge(s_res, groups_done(g, 3, 4))
                        for j in range(BG - (spare if g == 1 else 0)):
                            pool.indirect_dma_start(
                                out=out_v, out_offset=bass.IndirectOffsetOnAxis(ap=ids[g][:, j:j + 1], axis=0),
                                in_=res[g][:, j, :], in_offset=None, bounds_check=TOK - 1,
                                oob_is_err=False).then_inc(s_out, 16)

                    if not prev:
                        pool.wait_ge(s_w, 64)
                    for k in range(NB):
                        if group_at(k, 4) is not None:
                            send(group_at(k, 4))
                        if now(k, ROWS_LAG):
                            add_bias(k - ROWS_LAG)
                    if prev:
                        rows_out()
            clear_all()

        expert_turn(0, units=True, prev=False)
        with nc.Fori(1, TURNS) as it:
            expert_turn(it, units=True, prev=True)
        expert_turn(TURNS, units=False, prev=True)


def kernel(**inputs):
    import numpy as _np
    import concourse.bacc as _bacc
    from concourse import mybir as _mybir
    from concourse.bass_utils import run_bass_kernel_spmd as _run

    a = {k: _np.asarray(v) for k, v in inputs.items()}
    tr = lambda m: _np.ascontiguousarray(_np.swapaxes(m, -1, -2))
    laid = [
        ("x", a["L0_attn_x"]),
        ("w_all", _np.ascontiguousarray(_np.concatenate(
            [tr(a["L0_attn_Wqkv"]), tr(a["L0_attn_Walpha"]), tr(a["L0_attn_Wimp"])], axis=1))),
        ("b_all", _np.concatenate([a["L0_attn_bqkv"], a["L0_attn_balpha"], a["L0_attn_bimp"]])),
        ("wout_t", tr(a["L0_attn_Wout"])),
        ("bout", a["L0_attn_bout"]),
        ("thr", a["L0_attn_spike_threshold"].reshape(1)),
        ("log_k", a["L0_attn_log_k"]),
        ("qk_scale", a["L0_attn_qk_scale"].reshape(1)),
        ("wr_t", tr(a["L0_ffn_Wr"])),
        ("w1", a["L0_ffn_W1"]),
        ("b1", a["L0_ffn_b1"]),
        ("wo", a["L0_ffn_Wo"]),
        ("bo", a["L0_ffn_bo"]),
        ("gamma", a["L0_ffn_gamma"]),
        ("beta", a["L0_ffn_beta"]),
    ]
    nc = _bacc.Bacc("TRN2", target_bir_lowering=False, num_devices=1)
    arrays, args = {}, []
    for name, v in laid:
        v = _np.ascontiguousarray(v)
        arrays[f"in_{name}"] = v
        args.append(nc.dram_tensor(f"in_{name}", v.shape, _mybir.dt.from_np(v.dtype), kind="ExternalInput").ap())
    args.append(nc.dram_tensor("out_x", (B, T, C), F32, kind="ExternalOutput").ap())
    sandwich_kernel(nc, *args)
    r = _run(nc, [arrays], core_ids=[0])
    return r.results[0]["out_x"]
```
